# Optimizing a Trainium2 kernel written in Bass

```python
import numpy as np
import jax
import jax.numpy as jnp

def _softmax(x, axis=-1):
    return jax.nn.softmax(x, axis=axis)

def _gelu(x):
    return jax.nn.gelu(x, approximate=True)

def _silu(x):
    return jax.nn.silu(x)

def _sigmoid(x):
    return jax.nn.sigmoid(x)

def _layernorm(x, axis=-1, eps=1e-05):
    m = jnp.mean(x, axis=axis, keepdims=True)
    v = jnp.var(x, axis=axis, keepdims=True)
    return (x - m) / jnp.sqrt(v + eps)

def _scatter_add(tgt, idx, src, axis=0):
    return tgt.at[idx].add(src)

def _segment_sum(src, seg, n):
    return jax.ops.segment_sum(src, seg, n)
kernel_name = 'mk_xattn_ffn_d2_seqx_r8_f54353'

def setup_inputs(seed: int=0):
    np.random.seed(seed)
    _w = jnp.asarray

    def _rec_inputs():
        import jax
        import jax.numpy as jnp
        _rk = jax.random.key(seed)
        x = 4.136e-05 + 0.9999 * jax.random.normal(jax.random.fold_in(_rk, 1), (4, 256, 256), jnp.float32)
        _lenS = 256 - jax.random.randint(jax.random.fold_in(_rk, 7), (4,), 0, max(1, 256 // 4) + 1, jnp.int32)
        _lenS2 = 256 - jax.random.randint(jax.random.fold_in(_rk, 8), (4,), 0, max(1, 256 // 4) + 1, jnp.int32)
        _ctx_1024P = jax.random.normal(jax.random.fold_in(_rk, 11), (4, 16, 128), jnp.float32)
        _ctx_1024c = jax.random.dirichlet(jax.random.fold_in(_rk, 511), 0.3 * jnp.ones((16,), jnp.float32), (4, 256))
        _ctx_1024t = jnp.einsum('bsk,bkd->bsd', _ctx_1024c, _ctx_1024P)
        _ctx_1024t = _ctx_1024t * jax.lax.rsqrt(jnp.mean(jnp.square(_ctx_1024t)) + 1e-12) * 0.953939
        ctx_1024 = -0.000292821 + 1.00034 * (_ctx_1024t + 0.3 * jax.random.normal(jax.random.fold_in(_rk, 611), (4, 256, 128), jnp.float32))
        return (x, ctx_1024)
    x, ctx_1024 = _rec_inputs()

    def _L0_xattn_setup():
        import jax, jax.numpy as jnp
        import numpy as np
        import math
        B, L, DM = (2, 256, 128)
        DS, DC, EXP = (16, 4, 2)
        DI = EXP * DM
        DR = math.ceil(DM / 16)
        DT_MIN, DT_MAX, DT_FLOOR = (0.001, 0.1, 0.0001)

        def _ssm_forward(hidden_states, z, in_proj_w, conv_w, conv_b, x_proj_w, dt_proj_w, dt_proj_b, A_log, D):
            b = hidden_states.shape[0]
            x = jnp.einsum('ed,bld->bel', in_proj_w, hidden_states)
            xp = jnp.pad(x, ((0, 0), (0, 0), (DC - 1, 0)))
            xc = jax.lax.conv_general_dilated(xp, conv_w[:, None, :], window_strides=(1,), padding='VALID', dimension_numbers=('NCH', 'OIH', 'NCH'), feature_group_count=DI)
            u = jax.nn.silu(xc + conv_b[None, :, None])
            x_dbl = jnp.einsum('ke,bel->bkl', x_proj_w, u)
            dt_lo = x_dbl[:, :DR]
            Bm = x_dbl[:, DR:DR + DS]
            Cm = x_dbl[:, DR + DS:]
            delta = jax.nn.softplus(jnp.einsum('er,brl->bel', dt_proj_w, dt_lo) + dt_proj_b[None, :, None])
            A = -jnp.exp(A_log)

            def step(state, xs):
                d_t, B_t, C_t, u_t = xs
                dA = jnp.exp(d_t[..., None] * A)
                state = state * dA + (d_t * u_t)[..., None] * B_t[:, None, :]
                y_t = jnp.einsum('ben,bn->be', state, C_t)
                return (state, y_t)
            xs = (jnp.moveaxis(delta, -1, 0), jnp.moveaxis(Bm, -1, 0), jnp.moveaxis(Cm, -1, 0), jnp.moveaxis(u, -1, 0))
            state0 = jnp.zeros((b, DI, DS), delta.dtype)
            _, ys = jax.lax.scan(step, state0, xs)
            y = jnp.moveaxis(ys, 0, -1)
            y = y + D[None, :, None] * u
            y = y * jax.nn.silu(z)
            return jnp.swapaxes(y, 1, 2)
        key = jax.random.key(seed)
        ks = jax.random.split(key, 8)
        hidden_states = jax.random.normal(ks[0], (B, L, DM), jnp.float32)
        z = jax.random.normal(ks[1], (B, DI, L), jnp.float32)
        in_proj_w = jax.random.normal(ks[2], (DI, DM), jnp.float32) * DM ** (-0.5)
        conv_w = jax.random.normal(ks[3], (DI, DC), jnp.float32) * DC ** (-0.5)
        conv_b = jnp.zeros((DI,), jnp.float32)
        x_proj_w = jax.random.normal(ks[4], (DR + 2 * DS, DI), jnp.float32) * DI ** (-0.5)
        dt_std = DR ** (-0.5)
        dt_proj_w = jax.random.uniform(ks[5], (DI, DR), jnp.float32, -dt_std, dt_std)
        dt = jnp.exp(jax.random.uniform(ks[6], (DI,), jnp.float32) * (math.log(DT_MAX) - math.log(DT_MIN)) + math.log(DT_MIN))
        dt = jnp.clip(dt, DT_FLOOR)
        dt_proj_b = dt + jnp.log(-jnp.expm1(-dt))
        A_log = jnp.log(jnp.broadcast_to(jnp.arange(1, DS + 1, dtype=jnp.float32), (DI, DS)))
        D = jnp.ones((DI,), jnp.float32)
        return dict(hidden_states=hidden_states, z=z, in_proj_w=in_proj_w, conv_w=conv_w, conv_b=conv_b, x_proj_w=x_proj_w, dt_proj_w=dt_proj_w, dt_proj_b=dt_proj_b, A_log=A_log, D=D)
    _L0_xattn_all = _L0_xattn_setup()
    _L0_xattn_in = {k: v for k, v in _L0_xattn_all.items() if k in ('in_proj_w', 'conv_w', 'conv_b', 'x_proj_w', 'dt_proj_w', 'dt_proj_b', 'A_log', 'D')}
    del _L0_xattn_all

    def _L0_ffn_setup():
        import jax, jax.numpy as jnp
        import numpy as np
        DIM_IN = 256
        DIM_HIDDEN = 1024
        key = jax.random.key(seed)
        k_x, k_g, k_u, k_d = jax.random.split(key, 4)
        s_in = 1.0 / np.sqrt(DIM_IN)
        s_hid = 1.0 / np.sqrt(DIM_HIDDEN)
        x = jax.random.normal(k_x, (4, 256, DIM_IN), dtype=jnp.float32)
        w_gate = jax.random.uniform(k_g, (DIM_HIDDEN, DIM_IN), jnp.float32, -s_in, s_in)
        w_up = jax.random.uniform(k_u, (DIM_HIDDEN, DIM_IN), jnp.float32, -s_in, s_in)
        w_down = jax.random.uniform(k_d, (DIM_IN, DIM_HIDDEN), jnp.float32, -s_hid, s_hid)
        return {'x': x, 'w_gate': w_gate, 'w_up': w_up, 'w_down': w_down}
    _L0_ffn_all = _L0_ffn_setup()
    _L0_ffn_in = {k: v for k, v in _L0_ffn_all.items() if k in ('w_gate', 'w_up', 'w_down')}
    del _L0_ffn_all

    def _L1_xattn_setup():
        import jax, jax.numpy as jnp
        import numpy as np
        B_, L_, D_MODEL = (4, 256, 128)
        D_STATE, D_CONV, EXPAND = (16, 4, 2)
        D_INNER = EXPAND * D_MODEL
        DT_RANK = (D_MODEL + 15) // 16

        def silu(x):
            return x * jax.nn.sigmoid(x)
        key = jax.random.key(seed)
        ks = jax.random.split(key, 10)
        f32 = jnp.float32
        hidden_states = jax.random.normal(ks[0], (B_, L_, D_MODEL), dtype=f32)
        z = jax.random.normal(ks[1], (B_, D_INNER, L_), dtype=f32)
        in_proj_w = jax.random.normal(ks[2], (D_INNER, D_MODEL), dtype=f32) * 0.02
        conv_w = jax.random.normal(ks[3], (D_INNER, 1, D_CONV), dtype=f32) * 0.1
        conv_b = jax.random.normal(ks[4], (D_INNER,), dtype=f32) * 0.02
        x_proj_w = jax.random.normal(ks[5], (DT_RANK + 2 * D_STATE, D_INNER), dtype=f32) * 0.02
        dt_proj_w = jax.random.uniform(ks[6], (D_INNER, DT_RANK), dtype=f32, minval=-DT_RANK ** (-0.5), maxval=DT_RANK ** (-0.5))
        dt = jnp.exp(jax.random.uniform(ks[7], (D_INNER,), dtype=f32, minval=np.log(0.001), maxval=np.log(0.1)))
        dt_proj_b = jnp.log(jnp.expm1(dt))
        A_log = jnp.log(jnp.broadcast_to(jnp.arange(1, D_STATE + 1, dtype=f32), (D_INNER, D_STATE)))
        D = jnp.ones((D_INNER,), f32)
        return {'hidden_states': hidden_states, 'z': z, 'in_proj_w': in_proj_w, 'conv_w': conv_w, 'conv_b': conv_b, 'x_proj_w': x_proj_w, 'dt_proj_w': dt_proj_w, 'dt_proj_b': dt_proj_b, 'A_log': A_log, 'D': D}
    _L1_xattn_all = _L1_xattn_setup()
    _L1_xattn_in = {k: v for k, v in _L1_xattn_all.items() if k in ('in_proj_w', 'conv_w', 'conv_b', 'x_proj_w', 'dt_proj_w', 'dt_proj_b', 'A_log', 'D')}
    del _L1_xattn_all

    def _L1_ffn_setup():
        import jax, jax.numpy as jnp
        import numpy as np
        B, T, C = (4, 256, 256)
        E, K, I = (8, 2, 176)
        key = jax.random.key(seed)
        k0, k1, k2, k3, k4 = jax.random.split(key, 5)
        s = 0.02
        x = jax.random.normal(k0, (B, T, C), dtype=jnp.float32)
        gate_w = jax.random.normal(k1, (C, E), dtype=jnp.float32) * s
        w1 = jax.random.normal(k2, (E, C, I), dtype=jnp.float32) * s
        w3 = jax.random.normal(k3, (E, C, I), dtype=jnp.float32) * s
        w2 = jax.random.normal(k4, (E, I, C), dtype=jnp.float32) * s
        return {'x': x, 'gate_w': gate_w, 'w1': w1, 'w3': w3, 'w2': w2}
    _L1_ffn_all = _L1_ffn_setup()
    _L1_ffn_in = {k: v for k, v in _L1_ffn_all.items() if k in ('gate_w', 'w1', 'w3', 'w2')}
    del _L1_ffn_all
    return {'x': x, 'ctx_1024': ctx_1024, 'L0_xattn_in_proj_w': _L0_xattn_in['in_proj_w'], 'L0_xattn_conv_w': _L0_xattn_in['conv_w'], 'L0_xattn_conv_b': _L0_xattn_in['conv_b'], 'L0_xattn_x_proj_w': _L0_xattn_in['x_proj_w'], 'L0_xattn_dt_proj_w': _L0_xattn_in['dt_proj_w'], 'L0_xattn_dt_proj_b': _L0_xattn_in['dt_proj_b'], 'L0_xattn_A_log': _L0_xattn_in['A_log'], 'L0_xattn_D': _L0_xattn_in['D'], 'L0_ffn_w_gate': _L0_ffn_in['w_gate'], 'L0_ffn_w_up': _L0_ffn_in['w_up'], 'L0_ffn_w_down': _L0_ffn_in['w_down'], 'L1_xattn_in_proj_w': _L1_xattn_in['in_proj_w'], 'L1_xattn_conv_w': _L1_xattn_in['conv_w'], 'L1_xattn_conv_b': _L1_xattn_in['conv_b'], 'L1_xattn_x_proj_w': _L1_xattn_in['x_proj_w'], 'L1_xattn_dt_proj_w': _L1_xattn_in['dt_proj_w'], 'L1_xattn_dt_proj_b': _L1_xattn_in['dt_proj_b'], 'L1_xattn_A_log': _L1_xattn_in['A_log'], 'L1_xattn_D': _L1_xattn_in['D'], 'L1_ffn_gate_w': _L1_ffn_in['gate_w'], 'L1_ffn_w1': _L1_ffn_in['w1'], 'L1_ffn_w3': _L1_ffn_in['w3'], 'L1_ffn_w2': _L1_ffn_in['w2']}

def reference(x, ctx_1024, L0_xattn_in_proj_w, L0_xattn_conv_w, L0_xattn_conv_b, L0_xattn_x_proj_w, L0_xattn_dt_proj_w, L0_xattn_dt_proj_b, L0_xattn_A_log, L0_xattn_D, L0_ffn_w_gate, L0_ffn_w_up, L0_ffn_w_down, L1_xattn_in_proj_w, L1_xattn_conv_w, L1_xattn_conv_b, L1_xattn_x_proj_w, L1_xattn_dt_proj_w, L1_xattn_dt_proj_b, L1_xattn_A_log, L1_xattn_D, L1_ffn_gate_w, L1_ffn_w1, L1_ffn_w3, L1_ffn_w2):
    import jax
    import jax.numpy as jnp

    def _L0_xattn_ref(hidden_states, z, in_proj_w, conv_w, conv_b, x_proj_w, dt_proj_w, dt_proj_b, A_log, D):
        import jax, jax.numpy as jnp
        import numpy as np
        import math
        B, L, DM = (2, 256, 128)
        DS, DC, EXP = (16, 4, 2)
        DI = EXP * DM
        DR = math.ceil(DM / 16)
        DT_MIN, DT_MAX, DT_FLOOR = (0.001, 0.1, 0.0001)

        def _ssm_forward(hidden_states, z, in_proj_w, conv_w, conv_b, x_proj_w, dt_proj_w, dt_proj_b, A_log, D):
            b = hidden_states.shape[0]
            x = jnp.einsum('ed,bld->bel', in_proj_w, hidden_states)
            xp = jnp.pad(x, ((0, 0), (0, 0), (DC - 1, 0)))
            xc = jax.lax.conv_general_dilated(xp, conv_w[:, None, :], window_strides=(1,), padding='VALID', dimension_numbers=('NCH', 'OIH', 'NCH'), feature_group_count=DI)
            u = jax.nn.silu(xc + conv_b[None, :, None])
            x_dbl = jnp.einsum('ke,bel->bkl', x_proj_w, u)
            dt_lo = x_dbl[:, :DR]
            Bm = x_dbl[:, DR:DR + DS]
            Cm = x_dbl[:, DR + DS:]
            delta = jax.nn.softplus(jnp.einsum('er,brl->bel', dt_proj_w, dt_lo) + dt_proj_b[None, :, None])
            A = -jnp.exp(A_log)

            def step(state, xs):
                d_t, B_t, C_t, u_t = xs
                dA = jnp.exp(d_t[..., None] * A)
                state = state * dA + (d_t * u_t)[..., None] * B_t[:, None, :]
                y_t = jnp.einsum('ben,bn->be', state, C_t)
                return (state, y_t)
            xs = (jnp.moveaxis(delta, -1, 0), jnp.moveaxis(Bm, -1, 0), jnp.moveaxis(Cm, -1, 0), jnp.moveaxis(u, -1, 0))
            state0 = jnp.zeros((b, DI, DS), delta.dtype)
            _, ys = jax.lax.scan(step, state0, xs)
            y = jnp.moveaxis(ys, 0, -1)
            y = y + D[None, :, None] * u
            y = y * jax.nn.silu(z)
            return jnp.swapaxes(y, 1, 2)
        return _ssm_forward(hidden_states, z, in_proj_w, conv_w, conv_b, x_proj_w, dt_proj_w, dt_proj_b, A_log, D)

    def _L0_ffn_ref(x, w_gate, w_up, w_down):
        import jax, jax.numpy as jnp
        import numpy as np
        DIM_IN = 256
        DIM_HIDDEN = 1024
        gate = jnp.einsum('bsd,hd->bsh', x, w_gate)
        up = jnp.einsum('bsd,hd->bsh', x, w_up)
        gated = jax.nn.silu(gate) * up
        return jnp.einsum('bsh,dh->bsd', gated, w_down)

    def _L1_xattn_ref(hidden_states, z, in_proj_w, conv_w, conv_b, x_proj_w, dt_proj_w, dt_proj_b, A_log, D):
        import jax, jax.numpy as jnp
        import numpy as np
        B_, L_, D_MODEL = (4, 256, 128)
        D_STATE, D_CONV, EXPAND = (16, 4, 2)
        D_INNER = EXPAND * D_MODEL
        DT_RANK = (D_MODEL + 15) // 16

        def silu(x):
            return x * jax.nn.sigmoid(x)
        Bsz, L, _ = hidden_states.shape
        d_inner, _, d_conv = conv_w.shape
        dt_rank = dt_proj_w.shape[1]
        d_state = A_log.shape[1]
        x = jnp.einsum('bld,ed->bel', hidden_states, in_proj_w)
        xc = jax.lax.conv_general_dilated(x, conv_w, window_strides=(1,), padding=[(d_conv - 1, 0)], feature_group_count=d_inner, dimension_numbers=('NCH', 'OIH', 'NCH'))
        x = silu(xc + conv_b[None, :, None])
        x_dbl = jnp.einsum('bdl,ed->bel', x, x_proj_w)
        dt_low, Bm, Cm = jnp.split(x_dbl, [dt_rank, dt_rank + d_state], axis=1)
        dt = jnp.einsum('brl,dr->bdl', dt_low, dt_proj_w)
        dt = jax.nn.softplus(dt + dt_proj_b[None, :, None])
        A = -jnp.exp(A_log)
        dt_t = jnp.moveaxis(dt, -1, 0)
        B_t = jnp.moveaxis(Bm, -1, 0)
        C_t = jnp.moveaxis(Cm, -1, 0)
        u_t = jnp.moveaxis(x, -1, 0)

        def step(state, inp):
            d, b, c, u = inp
            dA = jnp.exp(d[..., None] * A)
            state = state * dA + (d * u)[..., None] * b[:, None, :]
            y = jnp.einsum('bdn,bn->bd', state, c)
            return (state, y)
        state0 = jnp.zeros((Bsz, d_inner, d_state), x.dtype)
        _, ys = jax.lax.scan(step, state0, (dt_t, B_t, C_t, u_t))
        y = jnp.moveaxis(ys, 0, 2)
        y = y + D[None, :, None] * x
        y = y * silu(z)
        return jnp.swapaxes(y, 1, 2)

    def _L1_ffn_ref(x, gate_w, w1, w3, w2):
        import jax, jax.numpy as jnp
        import numpy as np
        B, T, C = (4, 256, 256)
        E, K, I = (8, 2, 176)
        b, t, c = x.shape
        n_expert = gate_w.shape[1]
        xf = x.reshape(-1, c)
        n = xf.shape[0]
        logits = xf @ gate_w
        top_p, top_i = jax.lax.top_k(logits, K)
        probs = jax.nn.softmax(top_p.astype(jnp.float32), axis=-1).astype(x.dtype)
        weights = jnp.zeros((n, n_expert), dtype=x.dtype)
        weights = weights.at[jnp.arange(n)[:, None], top_i].add(probs)
        y = jnp.zeros_like(xf)
        for e in range(n_expert):
            h = jax.nn.silu(xf @ w1[e]) * (xf @ w3[e])
            y = y + weights[:, e:e + 1] * (h @ w2[e])
        return y.reshape(b, t, c)
    x = x + _L0_xattn_ref(ctx_1024, _layernorm(x, axis=-1), L0_xattn_in_proj_w, L0_xattn_conv_w, L0_xattn_conv_b, L0_xattn_x_proj_w, L0_xattn_dt_proj_w, L0_xattn_dt_proj_b, L0_xattn_A_log, L0_xattn_D)
    x = x + _L0_ffn_ref(_layernorm(x, axis=-1), L0_ffn_w_gate, L0_ffn_w_up, L0_ffn_w_down)
    x = x + _L1_xattn_ref(ctx_1024, _layernorm(x, axis=-1), L1_xattn_in_proj_w, L1_xattn_conv_w, L1_xattn_conv_b, L1_xattn_x_proj_w, L1_xattn_dt_proj_w, L1_xattn_dt_proj_b, L1_xattn_A_log, L1_xattn_D)
    x = x + _L1_ffn_ref(_layernorm(x, axis=-1), L1_ffn_gate_w, L1_ffn_w1, L1_ffn_w3, L1_ffn_w2)
    return x

_drawn_inputs = setup_inputs


def setup_inputs(seed=0):
    import zlib

    import numpy as np

    out = dict(_drawn_inputs(seed))
    spreads = {'L0_xattn_conv_b': (0.0, 0.1), 'L0_xattn_D': (1.0, 0.2), 'L1_xattn_D': (1.0, 0.6)}
    factors = {'L0_xattn_dt_proj_w': 6.215,
     'L1_xattn_in_proj_w': 4.515,
     'L1_xattn_conv_w': 4.6,
     'L1_xattn_conv_b': 8.0,
     'L1_xattn_x_proj_w': 8.0,
     'L1_xattn_dt_proj_w': 8.0,
     'L1_xattn_dt_proj_b': 8.0,
     'L1_xattn_A_log': 8.0,
     'L1_ffn_gate_w': 7.088,
     'L1_ffn_w1': 6.214,
     'L1_ffn_w3': 6.148,
     'L1_ffn_w2': 6.109}
    for name, (base, spread) in spreads.items():
        noise = np.random.default_rng([zlib.crc32(name.encode()), seed]).standard_normal(out[name].shape)
        drawn = base * np.exp(spread * noise) if base else spread * noise
        out[name] = jnp.asarray(drawn.astype(out[name].dtype))
    for name, factor in factors.items():
        out[name] = (out[name] * factor).astype(out[name].dtype)
    return out
```

```python
import numpy as np
import concourse.bass as bass
from concourse import mybir
from contextlib import ExitStack

P = 128
B, L, DX = 4, 256, 256
TOK = B * L
CH = 512
NB = CH // L
NCH = TOK // CH
TT = CH // P
DM, DI, DS, DR, DC = 128, 256, 16, 8, 4
HV = DI // P
EB = P // DS
BH = P // EB
BP = HV * BH
NPASS = 2 * NCH
NBLK = NPASS * BP
KX = DX // P
HID = 1024
NE, EI = 8, 176
MOE = NE * EI
EPS = 1e-5
NPART = 3
PADW = DC - 1 + L

LEAD = 4
NDA, NHB = 5, 9
SUMLAG = 7


def tiles_of(p):
    return HID // P if p < NCH else MOE // P


def first_tile(p):
    return sum(tiles_of(i) for i in range(p))


def schedule():
    at = {}

    def put(slot, *step):
        at.setdefault(slot, []).append(step)

    for p in range(NPASS):
        s = BP * (p - 1)
        put(s + 0, "project", p)
        put(s + 1, "pad", p)
        put(s + 2, "conv", p, 0)
        put(s + 3, "conv", p, 1)
        put(s + 5, "conv_silu", p)
        put(s + 6, "project_bc", p)
        put(s + 7, "keep_bc", p)
        put(s + 8, "project_dt", p)
        put(s + 9, "dt_exp", p)
        put(s + 10, "delta", p)
        for q in range(2):
            put(s + 11 + q, "hi", p, q)
            put(s + 12 + q, "rest", p, q)
            put(s + 13 + q, "mid", p, q)
            put(s + 14 + q, "lo", p, q)
        s = BP * p
        put(s + 3, "gate_stats", p)
        put(s + 4, "gate_rstd", p)
        put(s + 5, "gate_shift", p)
        put(s + 6, "gate_silu", p)
        s = BP * (p + 1)
        put(s + 4, "turn_y", p)
        put(s + 5, "add_y", p)
        put(s + 6, "ffn_rstd", p)
        put(s + 7, "ffn_norm", p)
        put(s + 9, "turn_x", p)
        put(s + 10, "keep_xt", p)
        moe = p >= NCH
        if moe:
            put(s + 11, "route", p)
            put(s + 12, "top2", p)
            put(s + 13, "route_exp", p)
            put(s + 14, "route_w", p)
            put(s + 15, "turn_w", p)
            put(s + 16, "keep_w", p)
        n = tiles_of(p)
        for i in range(2 * n):
            k = s + (16 + (i * 3) // 4 if moe else 11 + i)
            put(k, "gate" if i % 2 == 0 else "up", p, i // 2)
            put(k + 1, "tanh" if i % 2 == 0 else "hidden", p, i // 2)
        k = s + (32 if moe else 28)
        for t in range(TT):
            put(k + t, "down", p, t)
        put(k + TT // 2, "add_down", p, 0)
        put(k + TT, "add_down", p, 1)
        put(k + TT, "store", p)
    return at


AT = schedule()
SLOTS = range(min(AT), max(AT) + 1)


def bank_uses():
    uses = []
    for slot in SLOTS:
        for step in AT.get(slot, []):
            kind, p = step[0], step[1]
            if kind in ("project", "project_dt"):
                uses += [(kind, p, h) for h in range(HV)]
            elif kind == "project_bc":
                uses += [(kind, p, i) for i in range(3)]
            elif kind in ("turn_y", "turn_x"):
                uses += [(kind, p, h) for h in range(2)]
            elif kind in ("route", "turn_w", "gate"):
                uses.append(step)
            elif kind == "up":
                uses.append(step)
                if p >= NCH:
                    uses.append(("weight",) + step[1:])
            elif kind == "down" and step[2] % 2 == 0:
                uses.append(("down", p, step[2] // 2))
    return {u: (n % 3, n // 3) for n, u in enumerate(uses)}


USE = bank_uses()


def build(nc, x, ctx_t, in_proj_t, channel, x_proj_t, dt_proj_t, a_log, w_gate_t, w_up_t, w_down_t,
          route_w, w1_t, w3_t, w2_t, sel_spread, sel_sum, perm, ident, sel_weight, small, out):
    f32, bf16, u32 = mybir.dt.float32, mybir.dt.bfloat16, mybir.dt.uint32
    ALU, ACT = mybir.AluOpType, mybir.ActivationFunctionType
    ctx = ExitStack()
    with ctx:
        def sb(name, shape, dt=f32):
            return ctx.enter_context(nc.sbuf_tensor(name, shape, dt))

        def sem(name):
            return ctx.enter_context(nc.semaphore(name))

        xs = sb("xs", [P, TOK // P, DX])
        ctxt = sb("ctxt", [P, TOK])
        inp = sb("inp", [P, 2, HV, P])
        chan = sb("chan", [P, 2, HV, 7])
        xpr = sb("xpr", [P, 2, HV, DR + 2 * DS])
        dtp = sb("dtp", [DR, 2, HV, P])
        alog = sb("alog", [P, 2, BP])
        wa, wb, wc = sb("wa", [P, KX * MOE]), sb("wb", [P, KX * MOE]), sb("wc", [P, MOE // P, DX])
        wg, wu = (w[:, 0:KX * HID].rearrange("p (k n) -> p k n", k=KX) for w in (wa, wb))
        w1, w3 = (w[:].rearrange("p (k n) -> p k n", k=KX) for w in (wa, wb))
        rw = sb("rw", [P, KX, NE])
        hid = sb("hid", [P, MOE // P, CH])
        sels32 = hid[0:NPART * 32, 4, :].rearrange("p (j n) -> p j n", j=4)
        selw32 = hid[0:NPART * NE, 0:3, :].rearrange("p a n -> p (a n)")[:, 0:MOE]
        sely = sb("sely", [P, 4, 32])
        prm = sb("prm", [P, P])
        idn = sb("idn", [P, P])
        sml = sb("sml", [P, NE + TT])
        sels = sb("sels", [NPART * 32, 4, P], bf16)
        selw = sb("selw", [NPART * NE, MOE], bf16)
        aneg = sb("aneg", [P, 2, BP])
        xbc = sb("xbc", [P, 2, HV, 2, EB, DS])
        dperm = sb("dperm", [P, 2, HV, P])
        xpad = sb("xpad", [P, HV, NB, PADW])
        conv = sb("conv", [P, HV, NB, L])
        u = sb("u", [P, 2, HV, CH])
        brep = sb("brep", [P, 2, CH])
        crep = sb("crep", [P, 2, CH])
        dtlo = sb("dtlo", [DR, CH])
        dtv = conv[:].rearrange("p h b l -> p (h b l)")
        dta = sb("dta", [P, HV * CH])
        dtt = sb("dtt", [P, HV * CH])
        dtl = sb("dtl", [P, HV * CH])
        val = sb("val", [P, 2, HV * CH])
        parts = sb("parts", [P, NPART, 2, HV, CH], bf16)
        stack = sb("stack", [NPART * 32, HV, 2, 4, CH], bf16)
        da = sb("da", [P, NDA, NB, L])
        hst = sb("hst", [P, NHB, CH])
        sz = sb("sz", [P, HV, CH])
        bns = [sb(f"bns{i}", [P, TT, 6]) for i in range(2)]
        mv = [sb(f"mv{i}", [P, TT, 2]) for i in range(2)]
        ve = [sb(f"ve{i}", [P, TT]) for i in range(2)]
        rstd = [sb(f"rstd{i}", [P, TT]) for i in range(2)]
        shift = sb("shift", [P, TT])
        xn = sb("xn", [P, TT, DX])
        xnt = sb("xnt", [P, KX, CH])
        th = sb("th", [P, 2, CH])
        lg = sb("lg", [P, TT, NE])
        top = sb("top", [P, TT, NE])
        tix = sb("tix", [P, TT, NE], u32)
        tif = sb("tif", [P, TT, 2])
        d21 = sb("d21", [P, TT])
        e21 = sb("e21", [P, TT])
        s21 = sb("s21", [P, TT])
        p1 = sb("p1", [P, TT])
        p2 = sb("p2", [P, TT])
        m1 = sb("m1", [P, TT, NE])
        m2 = sb("m2", [P, TT, NE])
        wtok = sb("wtok", [P, TT, NE])
        whb = sb("whb", [P, TT, NPART, NE], bf16)
        wr = sb("wr", [P, TT, 2, NE])
        wprt = sb("wprt", [P, TT, NPART, NE])
        wts = sb("wts", [NPART * NE, CH], bf16)

        def bank(name):
            return ctx.enter_context(nc.psum_tensor(name, [P, CH], f32))

        dps = [bank(f"dps{i}") for i in range(2)]
        ups = [bank(f"ups{i}") for i in range(2)]
        yps = bank("yps")
        gen = [bank(f"gen{i}") for i in range(3)]

        in_ctx, in_sel, in_x, in_ffn, in_moe, in_w = (sem(n) for n in (
            "in_ctx", "in_sel", "in_x", "in_ffn", "in_moe", "in_w"))
        consts_made, a_exp, a_made = sem("consts_made"), sem("a_exp"), sem("a_made")
        zeroed = sem("zeroed")
        bank_full = [sem(f"bank_full{i}") for i in range(3)]
        bank_read = [sem(f"bank_read{i}") for i in range(3)]
        convolved, u_ready = sem("convolved"), sem("u_ready")
        dt_ready, val_ready = sem("dt_ready"), sem("val_ready")
        hi_ready, rest_ready, mid_ready, lo_ready = (sem(n) for n in (
            "hi_ready", "rest_ready", "mid_ready", "lo_ready"))
        stacked = [sem(f"stacked{h}") for h in range(HV)]
        delta_spread, decayed, u_spread, weighted, scanned, c_weighted, y_summed, y_gated = (sem(n) for n in (
            "delta_spread", "decayed", "u_spread", "weighted", "scanned", "c_weighted", "y_summed", "y_gated"))
        gate_var, gate_rstd, gate_shift, gate_ready = (sem(n) for n in (
            "gate_var", "gate_rstd", "gate_shift", "gate_ready"))
        ffn_var, ffn_rstd, ffn_normed, tanh_ready = (sem(n) for n in (
            "ffn_var", "ffn_rstd", "ffn_normed", "tanh_ready"))
        routed, route_expd, weights_made = (sem(n) for n in ("routed", "route_expd", "weights_made"))
        stored = sem("stored")
        act_step, dve_step, pool_step = sem("act_step"), sem("dve_step"), sem("pool_step")

        block = ctx.enter_context(nc.Block())
        NIN = {"ctx": 5, "sel": 4, "x": 1, "ffn": 3, "moe": 4}

        def full(eng, use):
            b, n = USE[use]
            eng.wait_ge(bank_full[b], n + 1)
            return gen[b]

        def free(ins, use):
            ins.then_inc(bank_read[USE[use][0]], 1)

        def wait_read(eng, use):
            b, n = USE[use]
            eng.wait_ge(bank_read[b], n + 1)

        def wait_hidden(eng, n):
            p = max(i for i in range(NPASS) if first_tile(i) <= n)
            wait_read(eng, ("up" if p < NCH else "weight", p, n - first_tile(p)))

        def stack_parts(sync, p, h):
            sync.wait_ge(hi_ready, 2 * (p + 1))
            sync.wait_ge(mid_ready, 2 * (p + 1))
            sync.wait_ge(lo_ready, 2 * (p + 1))
            if p >= 1:
                sync.wait_ge(delta_spread, BP * (p - 1) + BH * (h + 1))
                sync.wait_ge(u_spread, BP * (p - 1) + BH * (h + 1))
            for k in range(NPART):
                for s in range(4):
                    sync.dma_start(stack[32 * k:32 * k + 32, h, :, s, :],
                                   parts[32 * s:32 * s + 32, k, :, h, :]).then_inc(stacked[h], 16)

        @block.sync
        def _(sync):
            sync.dma_start(ctxt[:], ctx_t).then_inc(in_ctx, 16)
            sync.dma_start(inp[:], in_proj_t).then_inc(in_ctx, 16)
            sync.dma_start(chan[:], channel).then_inc(in_ctx, 16)
            sync.dma_start(xpr[:], x_proj_t).then_inc(in_ctx, 16)
            sync.dma_start(dtp[:], dt_proj_t).then_inc(in_ctx, 16)
            sync.dma_start(alog[:], a_log).then_inc(in_sel, 16)
            sync.dma_start(sels32, sel_spread).then_inc(in_sel, 16)
            sync.dma_start(sely[:], sel_sum).then_inc(in_sel, 16)
            sync.dma_start(prm[:], perm).then_inc(in_sel, 16)
            sync.dma_start(xs[:], x).then_inc(in_x, 16)
            sync.dma_start(idn[:], ident).then_inc(in_moe, 16)
            sync.dma_start(sml[:], small).then_inc(in_moe, 16)
            sync.dma_start(selw32, sel_weight).then_inc(in_moe, 16)
            sync.dma_start(rw[:], route_w).then_inc(in_moe, 16)
            sync.dma_start(wg, w_gate_t).then_inc(in_ffn, 16)
            sync.dma_start(wu, w_up_t).then_inc(in_ffn, 16)
            sync.dma_start(wc[:, 0:HID // P, :], w_down_t).then_inc(in_ffn, 16)
            for p in range(NPASS):
                for h in range(HV):
                    if p == NPASS - 1 and h == 1:
                        for w, to, use in ((w1_t, w1, ("gate", NCH - 1, HID // P - 1)),
                                           (w3_t, w3, ("up", NCH - 1, HID // P - 1)),
                                           (w2_t, wc[:], ("down", NCH - 1, 1))):
                            full(sync, use)
                            sync.dma_start(to, w).then_inc(in_w, 16)
                    stack_parts(sync, p, h)
            for c in range(NCH):
                for i in range(2):
                    p = NCH + c
                    wait_read(sync, ("down", p, i))
                    t = TT * c + 2 * i
                    sync.dma_start(out[:, t:t + 2, :], xs[:, t:t + 2, :]).then_inc(stored, 16)
            sync.wait_ge(stored, 16 * 2 * NCH)

        @block.tensor
        def _(pe):
            def claim(use):
                b, n = USE[use]
                if n >= 1:
                    pe.wait_ge(bank_read[b], n)
                return gen[b]

            def done(ins, use):
                ins.then_inc(bank_full[USE[use][0]], 1)

            def project(p):
                lay, c = divmod(p, NCH)
                if p == 0:
                    pe.wait_ge(in_ctx, 16 * NIN["ctx"])
                for h in range(HV):
                    ps = claim(("project", p, h))
                    done(nc.tensor.matmul(ps[:], inp[:, lay, h, :], ctxt[:, c * CH:(c + 1) * CH],
                                          start=True, stop=True), ("project", p, h))

            def project_bc(p):
                lay = p // NCH
                pe.wait_ge(u_ready, 2 * (p + 1))
                if p == 0:
                    pe.wait_ge(consts_made, 1)
                for i in range(3):
                    ps = claim(("project_bc", p, i))
                    for h in range(HV):
                        lhs = (xbc[:, lay, h, i].rearrange("p c n -> p (c n)") if i < 2
                               else xpr[:, lay, h, 0:DR])
                        o = ps[:] if i < 2 else ps[0:DR, :]
                        last = nc.tensor.matmul(o, lhs, u[:, p % 2, h, :], start=(h == 0), stop=(h == HV - 1))
                    done(last, ("project_bc", p, i))

            def project_dt(p):
                lay = p // NCH
                wait_read(pe, ("project_bc", p, 2))
                for h in range(HV):
                    ps = claim(("project_dt", p, h))
                    done(nc.tensor.matmul(ps[:], dtp[:, lay, h, :], dtlo[:], start=True, stop=True),
                         ("project_dt", p, h))

            def spread(k, quantity, banks, ready):
                p, b = divmod(k, BP)
                h, i = divmod(b, BH)
                s, j = divmod(i, 4)
                if i == 0:
                    pe.wait_ge(stacked[h], 16 * 4 * NPART * (p + 1))
                nc.tensor.matmul(banks[k % 2][:], sels[:, j, :], stack[:, h, quantity, s, :],
                                 start=True, stop=True).then_inc(ready, 1)

            def delta_block(k):
                if k >= 2:
                    pe.wait_ge(decayed, k - 1)
                spread(k, 0, dps, delta_spread)

            def u_block(k):
                if k >= 2:
                    pe.wait_ge(scanned, k - 1)
                spread(k, 1, ups, u_spread)

            def sum_batch(m):
                half = m // 4
                p, h = divmod(half, HV)
                s = m % 4
                if s == 0:
                    if half >= 1:
                        pe.wait_ge(y_gated, half)
                    if m == 0:
                        pe.wait_ge(consts_made, 2)
                    nc.tensor.matmul(yps[:], dperm[:, p // NCH, h, :], u[:, p % 2, h, :],
                                     start=True, stop=False, skip_group_check=True)
                pe.wait_ge(c_weighted, 4 * m + 4)
                for j in range(4):
                    last = nc.tensor.matmul(yps[32 * j:32 * j + 32, :], sely[:, s, :], hst[:, (4 * m + j) % NHB, :],
                                            start=False, stop=(s == 3), skip_group_check=True)
                last.then_inc(y_summed, 1)

            def turn_y(p):
                if p == 0:
                    pe.wait_ge(in_moe, 16 * NIN["moe"])
                pe.wait_ge(y_gated, 2 * (p + 1))
                for i in range(2):
                    ps = claim(("turn_y", p, i))
                    for t in range(2):
                        for h in range(HV):
                            last = nc.tensor.transpose(ps[:, t * DX + h * P:t * DX + (h + 1) * P],
                                                       sz[:, h, (2 * i + t) * P:(2 * i + t + 1) * P], idn[:])
                    done(last, ("turn_y", p, i))

            def turn_x(p):
                pe.wait_ge(ffn_normed, p + 1)
                for k in range(KX):
                    ps = claim(("turn_x", p, k))
                    for t in range(TT):
                        last = nc.tensor.transpose(ps[:, t * P:(t + 1) * P], xn[:, t, k * P:(k + 1) * P], idn[:])
                    done(last, ("turn_x", p, k))

            def route(p):
                for k in range(KX):
                    wait_read(pe, ("turn_x", p, k))
                ps = claim(("route", p))
                for t in range(TT):
                    for k in range(KX):
                        last = nc.tensor.matmul(ps[:, t * NE:(t + 1) * NE], xnt[:, k, t * P:(t + 1) * P],
                                                rw[:, k, :], start=(k == 0), stop=(k == KX - 1))
                done(last, ("route", p))

            def turn_w(p):
                pe.wait_ge(weights_made, p - NCH + 1)
                ps = claim(("turn_w", p))
                for t in range(TT):
                    last = nc.tensor.transpose(ps[0:NPART * NE, t * P:(t + 1) * P],
                                               wprt[:, t].rearrange("p k e -> p (k e)"), idn[:])
                done(last, ("turn_w", p))

            def gate_or_up(p, t, which):
                if which == "gate" and t == 0:
                    for k in range(KX):
                        wait_read(pe, ("turn_x", p, k))
                    if p == 0:
                        pe.wait_ge(in_ffn, 16 * NIN["ffn"])
                    if p == NCH:
                        pe.wait_ge(in_w, 16 * 3)
                w = ((wg, wu) if p < NCH else (w1, w3))[which == "up"]
                ps = claim((which, p, t))
                for k in range(KX):
                    last = nc.tensor.matmul(ps[:], w[:, k, t * P:(t + 1) * P], xnt[:, k, :],
                                            start=(k == 0), stop=(k == KX - 1))
                done(last, (which, p, t))

            def weight(p, t):
                if t == 0:
                    wait_read(pe, ("turn_w", p))
                ps = claim(("weight", p, t))
                done(nc.tensor.matmul(ps[:], selw[:, t * P:(t + 1) * P], wts[:], start=True, stop=True),
                     ("weight", p, t))

            def down(p, t):
                n = tiles_of(p)
                i, o = divmod(t, 2)
                if o == 0:
                    ps = claim(("down", p, i))
                    wait_hidden(pe, first_tile(p) + n - 1)
                else:
                    ps = gen[USE[("down", p, i)][0]]
                for k in range(n):
                    last = nc.tensor.matmul(ps[:, o * DX:(o + 1) * DX], hid[:, k, t * P:(t + 1) * P],
                                            wc[:, k, :], start=(k == 0), stop=(k == n - 1))
                if o == 1:
                    done(last, ("down", p, i))

            for slot in SLOTS:
                if 0 <= slot + LEAD < NBLK:
                    delta_block(slot + LEAD)
                if 0 <= slot + 2 < NBLK:
                    u_block(slot + 2)
                m, r = divmod(slot - SUMLAG, 4)
                if r == 0 and 0 <= m < NBLK // 4:
                    sum_batch(m)
                for kind, p, *at in AT.get(slot, []):
                    if kind == "project":
                        project(p)
                    elif kind == "project_bc":
                        project_bc(p)
                    elif kind == "project_dt":
                        project_dt(p)
                    elif kind == "turn_y":
                        turn_y(p)
                    elif kind == "turn_x":
                        turn_x(p)
                    elif kind == "route":
                        route(p)
                    elif kind == "turn_w":
                        turn_w(p)
                    elif kind == "gate":
                        gate_or_up(p, at[0], "gate")
                    elif kind == "up":
                        gate_or_up(p, at[0], "up")
                        if p >= NCH:
                            weight(p, at[0])
                    elif kind == "down":
                        down(p, at[0])

        @block.scalar
        def _(act):
            steps = [0]

            def then(ins):
                steps[0] += 1
                ins.then_inc(act_step, 1)
                act.wait_ge(act_step, steps[0])

            def pad(p):
                if p == 0:
                    act.wait_ge(zeroed, 1)
                for h in range(HV):
                    ps = full(act, ("project", p, h))
                    if p >= 1:
                        act.wait_ge(convolved, 2 * (p - 1) + h + 1)
                    ins = nc.scalar.activation(xpad[:, h, :, DC - 1:], ps[:].rearrange("p (b l) -> p b l", b=NB),
                                               ACT.Copy)
                    free(ins, ("project", p, h))

            def conv_silu(p):
                lay = p // NCH
                if p >= 2:
                    act.wait_ge(y_summed, 8 * (p - 2) + 5)
                for h in range(HV):
                    act.wait_ge(convolved, 2 * p + h + 1)
                    nc.scalar.activation(u[:, p % 2, h, :], conv[:, h].rearrange("p b l -> p (b l)"), ACT.Silu,
                                         bias=chan[:, lay, h, 4:5]).then_inc(u_ready, 1)

            def keep_bc(p):
                if p >= 2:
                    act.wait_ge(weighted, BP * (p - 1))
                    act.wait_ge(c_weighted, BP * (p - 1))
                for i, dst in enumerate((brep[:, p % 2, :], crep[:, p % 2, :], dtlo[:])):
                    ps = full(act, ("project_bc", p, i))
                    ins = nc.scalar.activation(dst, ps[:] if i < 2 else ps[0:DR, :], ACT.Copy)
                    free(ins, ("project_bc", p, i))

            def dt_exp(p):
                lay = p // NCH
                if p >= 1:
                    act.wait_ge(val_ready, 2 * p)
                for h in range(HV):
                    ps = full(act, ("project_dt", p, h))
                    ins = nc.scalar.activation(dtv[:, h * CH:(h + 1) * CH], ps[:], ACT.Identity,
                                               bias=chan[:, lay, h, 5:6])
                    free(ins, ("project_dt", p, h))
                for h in range(HV):
                    wait_read(act, ("project_dt", p, h))
                then(nc.scalar.activation(dta[:], dtv, ACT.Abs))
                then(nc.scalar.activation(dtt[:], dta[:], ACT.Exp, scale=-1.0))
                nc.scalar.activation(dtl[:], dtt[:], ACT.Ln, bias=1.0).then_inc(dt_ready, 1)

            def hi(p, q):
                act.wait_ge(val_ready, 2 * p + q + 1)
                if p >= 1:
                    for h in range(HV):
                        act.wait_ge(stacked[h], 16 * 4 * NPART * p)
                nc.scalar.activation(parts[:, 0, q].rearrange("p h t -> p (h t)"), val[:, q, :], ACT.Copy)\
                    .then_inc(hi_ready, 1)

            def mid(p, q):
                act.wait_ge(rest_ready, 2 * p + q + 1)
                nc.scalar.activation(parts[:, 1, q].rearrange("p h t -> p (h t)"), val[:, q, :], ACT.Copy)\
                    .then_inc(mid_ready, 1)

            def decay(k):
                p, b = divmod(k, BP)
                if k == 0:
                    act.wait_ge(a_made, 1)
                    act.wait_ge(zeroed, 2)
                if k >= NDA:
                    act.wait_ge(scanned, k - NDA + 1)
                act.wait_ge(delta_spread, k + 1)
                nc.scalar.activation(da[:, k % NDA, :, 1:], dps[k % 2][:].rearrange("p (b l) -> p b l", b=NB)[:, :, 1:],
                                     ACT.Exp, scale=aneg[:, p // NCH, b:b + 1]).then_inc(decayed, 1)

            def gate_silu(p):
                act.wait_ge(gate_shift, p + 1)
                if p >= 1:
                    full(act, ("turn_y", p - 1, 1))
                for t in range(TT):
                    b, h = divmod(t, HV)
                    nc.scalar.activation(sz[:, h, b * L:(b + 1) * L], xs[:, TT * (p % NCH) + t, :], ACT.Silu,
                                         bias=shift[:, t:t + 1], scale=rstd[0][:, t:t + 1]).then_inc(gate_ready, 1)

            def keep_xt(p):
                for k in range(KX):
                    ps = full(act, ("turn_x", p, k))
                    ins = nc.scalar.activation(xnt[:, k, :], ps[:], ACT.Copy)
                    free(ins, ("turn_x", p, k))

            def tanh(p, t):
                n = first_tile(p) + t
                ps = full(act, ("gate", p, t))
                if n >= 2:
                    wait_hidden(act, n - 2)
                nc.scalar.activation(th[:, n % 2, :], ps[:], ACT.Tanh, scale=0.5).then_inc(tanh_ready, 1)

            act.wait_ge(in_sel, 16 * NIN["sel"])
            nc.scalar.activation(aneg[:], alog[:], ACT.Exp).then_inc(a_exp, 1)
            for slot in SLOTS:
                if 0 <= slot + LEAD < NBLK:
                    decay(slot + LEAD)
                for kind, p, *at in AT.get(slot, []):
                    if kind == "pad":
                        pad(p)
                    elif kind == "conv_silu":
                        conv_silu(p)
                    elif kind == "keep_bc":
                        keep_bc(p)
                    elif kind == "dt_exp":
                        dt_exp(p)
                    elif kind == "hi":
                        hi(p, at[0])
                    elif kind == "mid":
                        mid(p, at[0])
                    elif kind == "gate_silu":
                        gate_silu(p)
                    elif kind == "keep_xt":
                        keep_xt(p)
                    elif kind == "tanh":
                        tanh(p, at[0])
                    elif kind == "route_exp":
                        act.wait_ge(routed, p - NCH + 1)
                        nc.scalar.activation(e21[:], d21[:], ACT.Exp).then_inc(route_expd, 1)
                    elif kind == "keep_w":
                        ps = full(act, ("turn_w", p))
                        ins = nc.scalar.activation(wts[:], ps[0:NPART * NE, :], ACT.Copy)
                        free(ins, ("turn_w", p))

        @block.vector
        def _(dve):
            steps = [0]

            def then(ins):
                steps[0] += 1
                ins.then_inc(dve_step, 1)
                dve.wait_ge(dve_step, steps[0])

            def taps(p, h):
                lay = p // NCH
                wait_read(dve, ("project", p, h))
                if p >= 1:
                    dve.wait_ge(u_ready, 2 * (p - 1) + h + 1)
                then(nc.vector.tensor_scalar(conv[:, h], xpad[:, h, :, 0:L], chan[:, lay, h, 0:1], None, ALU.mult))
                for k in range(1, DC):
                    ins = nc.vector.scalar_tensor_tensor(out=conv[:, h], in0=xpad[:, h, :, k:k + L],
                                                         scalar=chan[:, lay, h, k:k + 1], in1=conv[:, h],
                                                         op0=ALU.mult, op1=ALU.add)
                    if k < DC - 1:
                        then(ins)
                    else:
                        ins.then_inc(convolved, 1)

            def delta(p):
                dve.wait_ge(dt_ready, p + 1)
                if p >= 1:
                    dve.wait_ge(mid_ready, 2 * p)
                then(nc.vector.tensor_scalar(dta[:], dtt[:], 1.0, -1.0, ALU.add, ALU.add))
                then(nc.vector.tensor_tensor(dta[:], dtt[:], dta[:], ALU.subtract))
                then(nc.vector.tensor_tensor(dta[:], dta[:], dtl[:], ALU.add))
                then(nc.vector.scalar_tensor_tensor(out=val[:, 0, :], in0=dtv, scalar=0.0, in1=dta[:],
                                                    op0=ALU.max, op1=ALU.add))
                nc.vector.tensor_tensor(val[:, 1, :], val[:, 0, :], u[:, p % 2].rearrange("p h t -> p (h t)"),
                                        ALU.mult).then_inc(val_ready, 2)

            def rest_of(p, q):
                dve.wait_ge(hi_ready, 2 * p + q + 1)
                nc.vector.tensor_tensor(val[:, q, :], val[:, q, :], parts[:, 0, q].rearrange("p h t -> p (h t)"),
                                        ALU.subtract).then_inc(rest_ready, 1)

            def lo(p, q):
                dve.wait_ge(mid_ready, 2 * p + q + 1)
                nc.vector.tensor_tensor(parts[:, 2, q].rearrange("p h t -> p (h t)"), val[:, q, :],
                                        parts[:, 1, q].rearrange("p h t -> p (h t)"),
                                        ALU.subtract).then_inc(lo_ready, 1)

            def times_b(k):
                p = k // BP
                dve.wait_ge(u_spread, k + 1)
                if k % BP == 0:
                    wait_read(dve, ("project_bc", p, 0))
                nc.vector.tensor_tensor(ups[k % 2][:], ups[k % 2][:], brep[:, p % 2, :], ALU.mult)\
                    .then_inc(weighted, 1)

            def scan(k):
                dve.wait_ge(decayed, k + 1)
                dve.wait_ge(weighted, k + 1)
                if k >= NHB:
                    dve.wait_ge(y_summed, (k - NHB) // 4 + 1)
                nc.vector.tensor_tensor_scan(hst[:, k % NHB, :], da[:, k % NDA].rearrange("p b l -> p (b l)"),
                                             ups[k % 2][:], 0.0, ALU.mult, ALU.add).then_inc(scanned, 1)

            def gate_y(half):
                p, h = divmod(half, HV)
                dve.wait_ge(y_summed, 4 * half + 4)
                dve.wait_ge(gate_ready, TT * (p + 1))
                nc.vector.tensor_tensor(sz[:, h, :], yps[:], sz[:, h, :], ALU.mult).then_inc(y_gated, 1)

            def stats(which, tiles):
                for i, t in enumerate(tiles):
                    then(nc.vector.bn_stats(bns[which][:, i, :], xs[:, t, :]))
                    then(nc.vector.bn_aggr(mv[which][:, i, :], bns[which][:, i, :]))
                return nc.vector.tensor_scalar(ve[which][:], mv[which][:, :, 1], EPS, None, ALU.add)

            def gate_stats(p):
                if p == 0:
                    dve.wait_ge(in_x, 16 * NIN["x"])
                if p >= NCH:
                    for i in range(2):
                        wait_read(dve, ("down", p - NCH, i))
                stats(0, range(TT * (p % NCH), TT * (p % NCH + 1))).then_inc(gate_var, 1)

            def gate_shift_of(p):
                dve.wait_ge(gate_rstd, p + 1)
                if p >= 1:
                    dve.wait_ge(gate_ready, TT * p)
                nc.vector.scalar_tensor_tensor(out=shift[:], in0=mv[0][:, :, 0], scalar=-1.0, in1=rstd[0][:],
                                               op0=ALU.mult, op1=ALU.mult).then_inc(gate_shift, 1)

            def add_y(p):
                c = p % NCH
                for i in range(2):
                    ps = full(dve, ("turn_y", p, i))
                    t = TT * c + 2 * i
                    rows = xs[:, t:t + 2, :].rearrange("p a b -> p (a b)")
                    dve.wait_ge(gate_ready, TT * (p + 1))
                    ins = nc.vector.tensor_tensor(rows, ps[:], rows, ALU.add)
                    free(ins, ("turn_y", p, i))
                for i in range(2):
                    wait_read(dve, ("turn_y", p, i))
                stats(1, range(TT * c, TT * (c + 1))).then_inc(ffn_var, 1)

            def ffn_norm(p):
                c = p % NCH
                dve.wait_ge(ffn_rstd, p + 1)
                for t in range(TT):
                    ins = nc.vector.tensor_scalar(xn[:, t, :], xs[:, TT * c + t, :], mv[1][:, t, 0:1],
                                                  rstd[1][:, t:t + 1], ALU.subtract, ALU.mult)
                ins.then_inc(ffn_normed, 1)

            def hidden(p, t):
                n = first_tile(p) + t
                dve.wait_ge(tanh_ready, n + 1)
                ps = full(dve, ("gate", p, t))
                ins = nc.vector.scalar_tensor_tensor(out=th[:, n % 2, :], in0=th[:, n % 2, :], scalar=1.0, in1=ps[:],
                                                     op0=ALU.add, op1=ALU.mult)
                free(ins, ("gate", p, t))
                wait_read(dve, ("gate", p, t))
                ps = full(dve, ("up", p, t))
                dst = th[:, n % 2, :] if p >= NCH else hid[:, t, :]
                ins = nc.vector.scalar_tensor_tensor(out=dst, in0=th[:, n % 2, :], scalar=0.5, in1=ps[:],
                                                     op0=ALU.mult, op1=ALU.mult)
                free(ins, ("up", p, t))
                if p >= NCH:
                    wait_read(dve, ("up", p, t))
                    ps = full(dve, ("weight", p, t))
                    ins = nc.vector.tensor_tensor(hid[:, t, :], ps[:], th[:, n % 2, :], ALU.mult)
                    free(ins, ("weight", p, t))

            def add_down(p, i):
                ps = full(dve, ("down", p, i))
                t = TT * (p % NCH) + 2 * i
                rows = xs[:, t:t + 2, :].rearrange("p a b -> p (a b)")
                ins = nc.vector.tensor_tensor(rows, ps[:], rows, ALU.add)
                free(ins, ("down", p, i))

            def top2(p):
                ps = full(dve, ("route", p))
                ins = nc.vector.tensor_copy(lg[:].rearrange("p t e -> p (t e)"), ps[:, 0:TT * NE])
                free(ins, ("route", p))
                wait_read(dve, ("route", p))
                for t in range(TT):
                    then(nc.vector.max(top[:, t, :], lg[:, t, :]))
                    then(nc.vector.max_index(tix[:, t, :], top[:, t, :], lg[:, t, :]))
                then(nc.vector.tensor_copy(tif[:], tix[:, :, 0:2]))
                nc.vector.tensor_tensor(d21[:], top[:, :, 1], top[:, :, 0], ALU.subtract).then_inc(routed, 1)

            def route_weights(p):
                dve.wait_ge(route_expd, p - NCH + 1)
                then(nc.vector.tensor_scalar(s21[:], e21[:], 1.0, None, ALU.add))
                then(nc.vector.reciprocal(p1[:], s21[:]))
                then(nc.vector.tensor_tensor(p2[:], e21[:], p1[:], ALU.mult))
                for t in range(TT):
                    nc.vector.tensor_scalar(m1[:, t, :], sml[:, 0:NE], tif[:, t, 0:1], p1[:, t:t + 1],
                                            ALU.is_equal, ALU.mult)
                    ins = nc.vector.tensor_scalar(m2[:, t, :], sml[:, 0:NE], tif[:, t, 1:2], p2[:, t:t + 1],
                                                  ALU.is_equal, ALU.mult)
                then(ins)
                then(nc.vector.tensor_tensor(wtok[:], m1[:], m2[:], ALU.add))
                left = wtok[:]
                for k in range(NPART):
                    then(nc.vector.tensor_copy(whb[:, :, k, :], left))
                    if k < NPART - 1:
                        then(nc.vector.tensor_tensor(wr[:, :, k, :], left, whb[:, :, k, :], ALU.subtract))
                        left = wr[:, :, k, :]
                nc.vector.tensor_copy(wprt[:], whb[:]).then_inc(weights_made, 1)

            nc.vector.memset(xpad[:, :, :, 0:DC - 1], 0.0).then_inc(zeroed, 1)
            nc.vector.memset(da[:, :, :, 0:1], 0.0).then_inc(zeroed, 1)
            dve.wait_ge(in_ctx, 16 * NIN["ctx"])
            for lay in range(2):
                for h in range(HV):
                    for i in range(2):
                        cols = xpr[:, lay, h, DR + i * DS:DR + (i + 1) * DS]
                        ins = nc.vector.tensor_copy(xbc[:, lay, h, i],
                                                    cols.unsqueeze(1).to_broadcast([P, EB, DS]))
            ins.then_inc(consts_made, 1)
            dve.wait_ge(in_sel, 16 * NIN["sel"])
            nc.vector.tensor_copy(sels[:], sels32)
            for lay in range(2):
                for h in range(HV):
                    ins = nc.vector.tensor_scalar(dperm[:, lay, h, :], prm[:], chan[:, lay, h, 6:7], None, ALU.mult)
            ins.then_inc(consts_made, 1)
            dve.wait_ge(a_exp, 1)
            nc.vector.tensor_scalar(aneg[:], aneg[:], -1.0, None, ALU.mult).then_inc(a_made, 1)
            for slot in SLOTS:
                if 0 <= slot < NBLK:
                    scan(slot)
                if 0 <= slot + 1 < NBLK:
                    times_b(slot + 1)
                half, r = divmod(slot - BH - 4, BH)
                if r == 0 and 0 <= half < NBLK // BH:
                    gate_y(half)
                if slot == 0:
                    dve.wait_ge(in_moe, 16 * NIN["moe"])
                    nc.vector.tensor_copy(selw[:], selw32).then_inc(consts_made, 1)
                for kind, p, *at in AT.get(slot, []):
                    if kind == "conv":
                        taps(p, at[0])
                    elif kind == "delta":
                        delta(p)
                    elif kind == "rest":
                        rest_of(p, at[0])
                    elif kind == "lo":
                        lo(p, at[0])
                    elif kind == "gate_stats":
                        gate_stats(p)
                    elif kind == "gate_shift":
                        gate_shift_of(p)
                    elif kind == "add_y":
                        add_y(p)
                    elif kind == "ffn_norm":
                        ffn_norm(p)
                    elif kind == "top2":
                        top2(p)
                    elif kind == "route_w":
                        route_weights(p)
                    elif kind == "hidden":
                        hidden(p, at[0])
                    elif kind == "add_down":
                        add_down(p, at[0])

        @block.gpsimd
        def _(pool):
            def times_c(k):
                p = k // BP
                pool.wait_ge(scanned, k + 1)
                if k % BP == 0:
                    wait_read(pool, ("project_bc", p, 1))
                nc.gpsimd.tensor_tensor(hst[:, k % NHB, :], hst[:, k % NHB, :], crep[:, p % 2, :], ALU.mult)\
                    .then_inc(c_weighted, 1)

            def power(which, var, ready, n):
                pool.wait_ge(var, n + 1)
                if n == 0 and which == 0:
                    pool.wait_ge(in_moe, 16 * NIN["moe"])
                nc.gpsimd.tensor_tensor(rstd[which][:], ve[which][:], sml[:, NE:NE + TT], ALU.pow).then_inc(ready, 1)

            for slot in SLOTS:
                if 0 <= slot < NBLK:
                    times_c(slot)
                for kind, p, *at in AT.get(slot, []):
                    if kind == "gate_rstd":
                        power(0, gate_var, gate_rstd, p)
                    elif kind == "ffn_rstd":
                        power(1, ffn_var, ffn_rstd, p)


def kernel(**inputs):
    import concourse.bacc as bacc
    from concourse.bass_utils import run_bass_kernel_spmd

    a = {k: np.ascontiguousarray(v) for k, v in inputs.items()}
    f = np.float32
    q = np.arange(P)
    chan_of_q = 32 * (q // 8 % 4) + 8 * (q // 32) + q % 8
    order = np.concatenate([h * P + chan_of_q for h in range(HV)])
    layers = ("L0_xattn_", "L1_xattn_")

    def stacked(name, lay_out):
        return np.stack([lay_out(a[n + name]) for n in layers])

    def rows(w):
        return w[order].reshape(HV, P, -1).transpose(1, 0, 2)

    def k_tiles(w):
        return w.reshape(-1, P, w.shape[-1]).transpose(1, 0, 2)

    def by_block(w):
        return w[order].reshape(HV * BH, EB * DS).T

    arrays = {
        "x": k_tiles(a["x"].reshape(TOK, DX)),
        "ctx_t": a["ctx_1024"].reshape(TOK, DM).T,
        "in_proj_t": stacked("in_proj_w", lambda w: w[order].reshape(HV, P, DM).transpose(2, 0, 1)).transpose(1, 0, 2, 3),
        "channel": np.stack([np.concatenate(
            [rows(a[n + "conv_w"].reshape(DI, DC))] + [rows(a[n + m].reshape(DI, 1)) for m in ("conv_b", "dt_proj_b", "D")],
            axis=-1) for n in layers], axis=1),
        "x_proj_t": stacked("x_proj_w", lambda w: rows(w.T)).transpose(1, 0, 2, 3),
        "dt_proj_t": stacked("dt_proj_w", lambda w: w[order].reshape(HV, P, DR).transpose(2, 0, 1)).transpose(1, 0, 2, 3),
        "a_log": stacked("A_log", by_block).transpose(1, 0, 2),
        "w_gate_t": k_tiles(a["L0_ffn_w_gate"].T),
        "w_up_t": k_tiles(a["L0_ffn_w_up"].T),
        "w_down_t": k_tiles(a["L0_ffn_w_down"].T),
        "route_w": k_tiles(a["L1_ffn_gate_w"]),
        "w1_t": k_tiles(a["L1_ffn_w1"].transpose(1, 0, 2).reshape(DX, MOE)),
        "w3_t": k_tiles(a["L1_ffn_w3"].transpose(1, 0, 2).reshape(DX, MOE)),
        "w2_t": k_tiles(a["L1_ffn_w2"].reshape(MOE, DX)),
    }
    r = np.arange(NPART * 32)
    arrays["sel_spread"] = np.stack([(r[:, None] % 32 == EB * j + q[None, :] // DS) for j in range(4)], 1).astype(f)
    arrays["sel_sum"] = np.stack([(EB * s + q[:, None] // DS == np.arange(32)[None, :]) for s in range(4)], 1).astype(f)
    arrays["perm"] = (chan_of_q[:, None] == q[None, :]).astype(f)
    arrays["ident"] = np.eye(P, dtype=f)
    arrays["sel_weight"] = (np.arange(NPART * NE)[:, None] % NE == np.arange(MOE)[None, :] // EI).astype(f)
    arrays["small"] = np.concatenate([np.tile(np.arange(NE, dtype=f), (P, 1)), np.full((P, TT), -0.5, f)], axis=1)

    nc = bacc.Bacc("TRN2", target_bir_lowering=False, num_devices=1)
    arrays = {k: np.ascontiguousarray(v) for k, v in arrays.items()}
    args = [nc.dram_tensor(k, v.shape, mybir.dt.float32, kind="ExternalInput").ap() for k, v in arrays.items()]
    out = nc.dram_tensor("out", (P, TOK // P, DX), mybir.dt.float32, kind="ExternalOutput").ap()
    build(nc, *args, out)
    got = run_bass_kernel_spmd(nc, [arrays], core_ids=[0]).results[0]["out"]
    return np.ascontiguousarray(got.transpose(1, 0, 2)).reshape(B, L, DX)
```

```python
import numpy as np
import concourse.bass as bass
from concourse import mybir
from contextlib import ExitStack

P = 128
B, L, DX = 4, 256, 256
TOK = B * L
CH = 512
NB = CH // L
NCH = TOK // CH
TT = CH // P
DM, DI, DS, DR, DC = 128, 256, 16, 8, 4
HV = DI // P
EB = P // DS
BH = P // EB
BP = HV * BH
NPASS = 2 * NCH
NBLK = NPASS * BP
KX = DX // P
HID = 1024
NE, EI = 8, 176
MOE = NE * EI
EPS = 1e-5
NPART = 3
PADW = DC - 1 + L

LEAD = 4
NDA, NHB = 5, 9
SUMLAG = 7


def tiles_of(p):
    return HID // P if p < NCH else MOE // P


def first_tile(p):
    return sum(tiles_of(i) for i in range(p))


def schedule():
    at = {}

    def put(slot, *step):
        at.setdefault(slot, []).append(step)

    for p in range(NPASS):
        s = BP * (p - 1)
        put(s - 12, "project", p)
        put(s - 10, "pad", p)
        for k in range(DC):
            put(s - 8 + k, "tap", p, k)
        put(s - 3, "conv_silu", p)
        for i in range(3):
            put(s - 1 + i, "project_bc", p, i)
            put(s + 1 + i, "keep_bc", p, i)
        put(s + 4, "project_dt", p)
        put(s + 6, "dt_bias", p)
        put(s + 7, "dt_abs", p)
        put(s + 8, "dt_exp", p)
        put(s + 9, "dt_ln", p)
        put(s + 11, "round_up", p)
        for h, k in ((0, s + 12), (1, s + 14)):
            put(k, "lost", p, h)
            put(k + 1 + h, "log_sum", p, h)
            put(k + 2 + 2 * h, "delta", p, h)
            put(k + 4 + 2 * h, "delta_u", p, h)
        for (q, h), k in zip(((0, 0), (1, 0), (0, 1), (1, 1)), (s + 15, s + 17, s + 19, s + 21)):
            put(k, "hi", p, q, h)
            put(k + 2, "rest", p, q, h)
            put(k + 3, "mid", p, q, h)
            put(k + 5, "lo", p, q, h)
        s = BP * p
        put(s + 13, "gate_stats", p)
        put(s + 14, "gate_aggr", p)
        put(s + 15, "gate_rstd", p)
        put(s + 17, "gate_shift", p)
        put(s + 17, "gate_silu", p)
        s = BP * (p + 1)
        n, moe = tiles_of(p), p >= NCH
        put(s + 6, "turn_y", p)
        put(s + 7, "add_y", p)
        put(s + 8, "ffn_stats", p)
        put(s + 9, "ffn_aggr", p)
        put(s + 10, "ffn_rstd", p)
        put(s + 11, "ffn_norm", p)
        put(s + 12, "turn_x", p)
        put(s + 13, "keep_xt", p)
        busy = {BP * q + k for q in range(-1, NPASS - 1) for k in (BP - 12, BP - 1, BP, BP + 1, BP + 4)}
        free = (k for k in range(s + 14, s + 99) if k not in busy)
        for t in range(n):
            k = next(free)
            put(k, "gate", p, t)
            put(k, "tanh", p, t)
            put(k + 1, "silu", p, t)
            k = next(free)
            put(k, "up", p, t)
            put(k + 1, "hidden", p, t)
            if moe:
                j = max(s + 27 + t, k + 2)
                put(j, "weight", p, t)
                put(j + 1, "weigh", p, t)
                if t == n - 1:
                    next(free), next(free)
            elif t == n - 1:
                next(free)
        if moe:
            put(s + 15, "route", p)
            put(s + 16, "top2", p)
            put(s + 18, "route_exp", p)
            put(s + 20, "route_w", p)
            put(s + 23, "turn_w", p)
            put(s + 24, "keep_w", p)
        for t in range(TT):
            for part in range(2):
                k = next(free)
                put(k, "down", p, t, part)
            if t % 2:
                put(k + 1, "add_down", p, t // 2)
    return at


AT = schedule()
SLOTS = range(min(AT), max(AT) + 1)


READER = {"project": "pad", "project_bc": "keep_bc", "project_dt": "dt_bias", "turn_y": "add_y",
          "turn_x": "keep_xt", "route": "top2", "turn_w": "keep_w", "gate": "silu", "up": "hidden",
          "weight": "weigh", "down": "add_down"}


def bank_uses():
    slot_of = {step: slot for slot, steps in AT.items() for step in steps}
    uses, read, count = {}, [min(AT)] * 3, [0] * 3
    for slot in SLOTS:
        for kind, p, *at in AT.get(slot, []):
            if kind not in READER or (kind == "down" and (at[0] % 2 or at[1])):
                continue
            pair = kind in ("project", "project_dt", "turn_y", "turn_x")
            for i in range(2) if pair else (at[0] // 2,) if kind == "down" else at or (None,):
                use = (kind, p) if i is None else (kind, p, i)
                b = read.index(min(read))
                uses[use] = (b, count[b])
                count[b] += 1
                read[b] = slot_of[(READER[kind], p) if pair and kind != "down" else (READER[kind],) + use[1:]]
    return uses


USE = bank_uses()


def build(nc, x, ctx_t, in_proj_t, channel, x_proj_t, dt_proj_t, a_log, w_gate_t, w_up_t, w_down_t,
          route_w, w1_t, w3_t, w2_t, sel_spread, sel_sum, perm, ident, sel_weight, small, out):
    f32, bf16, u32 = mybir.dt.float32, mybir.dt.bfloat16, mybir.dt.uint32
    ALU, ACT = mybir.AluOpType, mybir.ActivationFunctionType
    ctx = ExitStack()
    with ctx:
        def sb(name, shape, dt=f32):
            return ctx.enter_context(nc.sbuf_tensor(name, shape, dt))

        def sem(name):
            return ctx.enter_context(nc.semaphore(name))

        xs = sb("xs", [P, TOK // P, DX])
        ctxt = sb("ctxt", [P, TOK])
        inp = sb("inp", [P, 2, HV, P])
        chan = sb("chan", [P, 2, HV, 7])
        xpr = sb("xpr", [P, 2, HV, DR + 2 * DS])
        dtp = sb("dtp", [DR, 2, HV, P])
        alog = sb("alog", [P, 2, BP])
        wa, wb, wc = sb("wa", [P, KX * MOE]), sb("wb", [P, KX * MOE]), sb("wc", [P, MOE // P, DX])
        wg, wu = (w[:, 0:KX * HID].rearrange("p (k n) -> p k n", k=KX) for w in (wa, wb))
        w1, w3 = (w[:].rearrange("p (k n) -> p k n", k=KX) for w in (wa, wb))
        rw = sb("rw", [P, KX, NE])
        hid = sb("hid", [P, MOE // P, CH])
        sels32 = hid[0:NPART * 32, 4, :].rearrange("p (j n) -> p j n", j=4)
        selw32 = hid[0:NPART * NE, 0:3, :].rearrange("p a n -> p (a n)")[:, 0:MOE]
        sely = sb("sely", [P, 4, 32])
        prm = sb("prm", [P, P])
        idn = sb("idn", [P, P])
        sml = sb("sml", [P, NE + TT])
        sels = sb("sels", [NPART * 32, 4, P], bf16)
        selw = sb("selw", [NPART * NE, MOE], bf16)
        aneg = sb("aneg", [P, 2, BP])
        xbc = sb("xbc", [P, 2, HV, 2, EB, DS])
        dperm = sb("dperm", [P, 2, HV, P])
        xpad = sb("xpad", [P, HV, NB, PADW])
        conv = sb("conv", [P, HV, NB, L])
        u = sb("u", [P, 2, HV, CH])
        brep = sb("brep", [P, 2, CH])
        crep = sb("crep", [P, 2, CH])
        dtlo = sb("dtlo", [DR, CH])
        dtv = conv[:].rearrange("p h b l -> p (h b l)")
        dtt = sb("dtt", [P, HV * CH])
        dtl = sb("dtl", [P, HV * CH])
        dta = sb("dta", [P, HV * CH])
        val = sb("val", [P, 2, HV, CH])
        parts = sb("parts", [P, NPART, 2, HV, CH], bf16)
        stack = sb("stack", [NPART * 32, HV, 2, 4, CH], bf16)
        da = sb("da", [P, NDA, NB, L])
        hst = sb("hst", [P, NHB, CH])
        sz = sb("sz", [P, HV, CH])
        bns = [sb(f"bns{i}", [P, TT, 6]) for i in range(2)]
        mv = [sb(f"mv{i}", [P, TT, 2]) for i in range(2)]
        ve = [sb(f"ve{i}", [P, TT]) for i in range(2)]
        rstd = [sb(f"rstd{i}", [P, TT]) for i in range(2)]
        shift = sb("shift", [P, TT])
        xn = sb("xn", [P, TT, DX])
        xnt = sb("xnt", [P, KX, CH])
        th = sb("th", [P, 2, CH])
        lg = sb("lg", [P, TT, NE])
        top = sb("top", [P, TT, NE])
        tix = sb("tix", [P, TT, NE], u32)
        tif = sb("tif", [P, TT, 2])
        d21 = sb("d21", [P, TT])
        e21 = sb("e21", [P, TT])
        s21 = sb("s21", [P, TT])
        p1 = sb("p1", [P, TT])
        p2 = sb("p2", [P, TT])
        m1 = sb("m1", [P, TT, NE])
        m2 = sb("m2", [P, TT, NE])
        wtok = sb("wtok", [P, TT, NE])
        whb = sb("whb", [P, TT, NPART, NE], bf16)
        wr = sb("wr", [P, TT, 2, NE])
        wprt = sb("wprt", [P, TT, NPART, NE])
        wts = sb("wts", [NPART * NE, CH], bf16)

        def bank(name):
            return ctx.enter_context(nc.psum_tensor(name, [P, CH], f32))

        dps = [bank(f"dps{i}") for i in range(2)]
        ups = [bank(f"ups{i}") for i in range(2)]
        yps = bank("yps")
        gen = [bank(f"gen{i}") for i in range(3)]

        in_ctx, in_sel, in_x, in_ffn, in_moe, in_w = (sem(n) for n in (
            "in_ctx", "in_sel", "in_x", "in_ffn", "in_moe", "in_w"))
        consts_made, a_exp, a_made = sem("consts_made"), sem("a_exp"), sem("a_made")
        zeroed = sem("zeroed")
        bank_full = [sem(f"bank_full{i}") for i in range(3)]
        bank_read = [sem(f"bank_read{i}") for i in range(3)]
        tapped, u_ready = sem("tapped"), sem("u_ready")
        abs_ready, exp_ready, ln_ready, rounded, lost_ready, log_summed = (sem(n) for n in (
            "abs_ready", "exp_ready", "ln_ready", "rounded", "lost_ready", "log_summed"))
        delta_ready, delta_u_ready = sem("delta_ready"), sem("delta_u_ready")
        hi_ready, rest_ready, mid_ready, lo_ready = (sem(n) for n in (
            "hi_ready", "rest_ready", "mid_ready", "lo_ready"))
        stacked = [sem(f"stacked{h}") for h in range(HV)]
        delta_spread, decayed, u_spread, weighted, scanned, c_weighted, y_summed, y_gated = (sem(n) for n in (
            "delta_spread", "decayed", "u_spread", "weighted", "scanned", "c_weighted", "y_summed", "y_gated"))
        stats_made, aggregated, var_ready, rstd_ready = (
            [sem(f"{n}_{norm}") for norm in ("gate", "ffn")]
            for n in ("stats_made", "aggregated", "var_ready", "rstd_ready"))
        gate_shift, gate_ready, ffn_normed, tanh_ready = (sem(n) for n in (
            "gate_shift", "gate_ready", "ffn_normed", "tanh_ready"))
        routed, route_expd, weights_made = (sem(n) for n in ("routed", "route_expd", "weights_made"))
        stored = sem("stored")
        act_step, dve_step, pool_step = sem("act_step"), sem("dve_step"), sem("pool_step")

        block = ctx.enter_context(nc.Block())
        NIN = {"ctx": 5, "sel": 4, "x": 1, "ffn": 3, "moe": 4}

        def full(eng, use):
            b, n = USE[use]
            eng.wait_ge(bank_full[b], n + 1)
            return gen[b]

        def free(ins, use):
            ins.then_inc(bank_read[USE[use][0]], 1)

        def wait_read(eng, use):
            b, n = USE[use]
            eng.wait_ge(bank_read[b], n + 1)

        def tile_use(kind, n):
            p = max(i for i in range(NPASS) if first_tile(i) <= n)
            return kind, p, n - first_tile(p)

        def order(p, q, h):
            return 4 * p + 2 * h + q + 1

        def stack_parts(sync, p, h):
            sync.wait_ge(hi_ready, order(p, 1, h))
            sync.wait_ge(mid_ready, order(p, 1, h))
            sync.wait_ge(lo_ready, order(p, 1, h))
            if p >= 1:
                sync.wait_ge(delta_spread, BP * (p - 1) + BH * (h + 1))
                sync.wait_ge(u_spread, BP * (p - 1) + BH * (h + 1))
            for k in range(NPART):
                for s in range(4):
                    sync.dma_start(stack[32 * k:32 * k + 32, h, :, s, :],
                                   parts[32 * s:32 * s + 32, k, :, h, :]).then_inc(stacked[h], 16)

        @block.sync
        def _(sync):
            sync.dma_start(ctxt[:], ctx_t).then_inc(in_ctx, 16)
            sync.dma_start(inp[:], in_proj_t).then_inc(in_ctx, 16)
            sync.dma_start(chan[:], channel).then_inc(in_ctx, 16)
            sync.dma_start(xpr[:], x_proj_t).then_inc(in_ctx, 16)
            sync.dma_start(dtp[:], dt_proj_t).then_inc(in_ctx, 16)
            sync.dma_start(alog[:], a_log).then_inc(in_sel, 16)
            sync.dma_start(sels32, sel_spread).then_inc(in_sel, 16)
            sync.dma_start(sely[:], sel_sum).then_inc(in_sel, 16)
            sync.dma_start(prm[:], perm).then_inc(in_sel, 16)
            sync.dma_start(xs[:], x).then_inc(in_x, 16)
            sync.dma_start(idn[:], ident).then_inc(in_moe, 16)
            sync.dma_start(sml[:], small).then_inc(in_moe, 16)
            sync.dma_start(selw32, sel_weight).then_inc(in_moe, 16)
            sync.dma_start(rw[:], route_w).then_inc(in_moe, 16)
            sync.dma_start(wg, w_gate_t).then_inc(in_ffn, 16)
            sync.dma_start(wu, w_up_t).then_inc(in_ffn, 16)
            sync.dma_start(wc[:, 0:HID // P, :], w_down_t).then_inc(in_ffn, 16)
            for p in range(NPASS):
                for h in range(HV):
                    if p == NPASS - 1 and h == 1:
                        for w, to, use in ((w1_t, w1, ("gate", NCH - 1, HID // P - 1)),
                                           (w3_t, w3, ("up", NCH - 1, HID // P - 1)),
                                           (w2_t, wc[:], ("down", NCH - 1, 1))):
                            full(sync, use)
                            sync.dma_start(to, w).then_inc(in_w, 16)
                    stack_parts(sync, p, h)
            for c in range(NCH):
                for i in range(2):
                    p = NCH + c
                    wait_read(sync, ("down", p, i))
                    t = TT * c + 2 * i
                    sync.dma_start(out[:, t:t + 2, :], xs[:, t:t + 2, :]).then_inc(stored, 16)
            sync.wait_ge(stored, 16 * 2 * NCH)

        @block.tensor
        def _(pe):
            def claim(use):
                b, n = USE[use]
                if n >= 1:
                    pe.wait_ge(bank_read[b], n)
                return gen[b]

            def done(ins, use):
                ins.then_inc(bank_full[USE[use][0]], 1)

            def project(p):
                lay, c = divmod(p, NCH)
                if p == 0:
                    pe.wait_ge(in_ctx, 16 * NIN["ctx"])
                for h in range(HV):
                    ps = claim(("project", p, h))
                    done(nc.tensor.matmul(ps[:], inp[:, lay, h, :], ctxt[:, c * CH:(c + 1) * CH],
                                          start=True, stop=True), ("project", p, h))

            def project_bc(p, i):
                lay = p // NCH
                if i == 0:
                    pe.wait_ge(u_ready, 2 * (p + 1))
                    if p == 0:
                        pe.wait_ge(consts_made, 1)
                ps = claim(("project_bc", p, i))
                for h in range(HV):
                    lhs = xbc[:, lay, h, i].rearrange("p c n -> p (c n)") if i < 2 else xpr[:, lay, h, 0:DR]
                    o = ps[:] if i < 2 else ps[0:DR, :]
                    last = nc.tensor.matmul(o, lhs, u[:, p % 2, h, :], start=(h == 0), stop=(h == HV - 1))
                done(last, ("project_bc", p, i))

            def project_dt(p):
                lay = p // NCH
                wait_read(pe, ("project_bc", p, 2))
                for h in range(HV):
                    ps = claim(("project_dt", p, h))
                    done(nc.tensor.matmul(ps[:], dtp[:, lay, h, :], dtlo[:], start=True, stop=True),
                         ("project_dt", p, h))

            def spread(k, quantity, banks, ready):
                p, b = divmod(k, BP)
                h, i = divmod(b, BH)
                s, j = divmod(i, 4)
                if i == 0:
                    pe.wait_ge(stacked[h], 16 * 4 * NPART * (p + 1))
                nc.tensor.matmul(banks[k % 2][:], sels[:, j, :], stack[:, h, quantity, s, :],
                                 start=True, stop=True).then_inc(ready, 1)

            def delta_block(k):
                if k >= 2:
                    pe.wait_ge(decayed, k - 1)
                spread(k, 0, dps, delta_spread)

            def u_block(k):
                if k >= 2:
                    pe.wait_ge(scanned, k - 1)
                spread(k, 1, ups, u_spread)

            def sum_batch(m):
                half = m // 4
                p, h = divmod(half, HV)
                s = m % 4
                if s == 0:
                    if half >= 1:
                        pe.wait_ge(y_gated, half)
                    if m == 0:
                        pe.wait_ge(consts_made, 2)
                    nc.tensor.matmul(yps[:], dperm[:, p // NCH, h, :], u[:, p % 2, h, :],
                                     start=True, stop=False, skip_group_check=True)
                pe.wait_ge(c_weighted, 4 * m + 4)
                for j in range(4):
                    last = nc.tensor.matmul(yps[32 * j:32 * j + 32, :], sely[:, s, :], hst[:, (4 * m + j) % NHB, :],
                                            start=False, stop=(s == 3), skip_group_check=True)
                last.then_inc(y_summed, 1)

            def turn_y(p):
                if p == 0:
                    pe.wait_ge(in_moe, 16 * NIN["moe"])
                pe.wait_ge(y_gated, 2 * (p + 1))
                for i in range(2):
                    ps = claim(("turn_y", p, i))
                    for t in range(2):
                        for h in range(HV):
                            last = nc.tensor.transpose(ps[:, t * DX + h * P:t * DX + (h + 1) * P],
                                                       sz[:, h, (2 * i + t) * P:(2 * i + t + 1) * P], idn[:])
                    done(last, ("turn_y", p, i))

            def turn_x(p):
                pe.wait_ge(ffn_normed, p + 1)
                for k in range(KX):
                    ps = claim(("turn_x", p, k))
                    for t in range(TT):
                        last = nc.tensor.transpose(ps[:, t * P:(t + 1) * P], xn[:, t, k * P:(k + 1) * P], idn[:])
                    done(last, ("turn_x", p, k))

            def route(p):
                for k in range(KX):
                    wait_read(pe, ("turn_x", p, k))
                ps = claim(("route", p))
                for t in range(TT):
                    for k in range(KX):
                        last = nc.tensor.matmul(ps[:, t * NE:(t + 1) * NE], xnt[:, k, t * P:(t + 1) * P],
                                                rw[:, k, :], start=(k == 0), stop=(k == KX - 1))
                done(last, ("route", p))

            def turn_w(p):
                pe.wait_ge(weights_made, p - NCH + 1)
                ps = claim(("turn_w", p))
                for t in range(TT):
                    last = nc.tensor.transpose(ps[0:NPART * NE, t * P:(t + 1) * P],
                                               wprt[:, t].rearrange("p k e -> p (k e)"), idn[:])
                done(last, ("turn_w", p))

            def gate_or_up(p, t, which):
                if which == "gate" and t == 0:
                    for k in range(KX):
                        wait_read(pe, ("turn_x", p, k))
                    if p == 0:
                        pe.wait_ge(in_ffn, 16 * NIN["ffn"])
                    if p == NCH:
                        pe.wait_ge(in_w, 16 * 3)
                w = ((wg, wu) if p < NCH else (w1, w3))[which == "up"]
                ps = claim((which, p, t))
                for k in range(KX):
                    last = nc.tensor.matmul(ps[:], w[:, k, t * P:(t + 1) * P], xnt[:, k, :],
                                            start=(k == 0), stop=(k == KX - 1))
                done(last, (which, p, t))

            def weight(p, t):
                if t == 0:
                    wait_read(pe, ("turn_w", p))
                ps = claim(("weight", p, t))
                done(nc.tensor.matmul(ps[:], selw[:, t * P:(t + 1) * P], wts[:], start=True, stop=True),
                     ("weight", p, t))

            def down(p, t, part):
                n = tiles_of(p)
                i, o = divmod(t, 2)
                if o == 0 and part == 0:
                    ps = claim(("down", p, i))
                    wait_read(pe, ("up" if p < NCH else "weight", p, n - 1))
                else:
                    ps = gen[USE[("down", p, i)][0]]
                for k in range(n // 2 * part, n if part else n // 2):
                    last = nc.tensor.matmul(ps[:, o * DX:(o + 1) * DX], hid[:, k, t * P:(t + 1) * P],
                                            wc[:, k, :], start=(k == 0), stop=(k == n - 1))
                if o == 1 and part == 1:
                    done(last, ("down", p, i))

            for slot in SLOTS:
                if 0 <= slot + LEAD < NBLK:
                    delta_block(slot + LEAD)
                m, r = divmod(slot - SUMLAG, 4)
                if r == 0 and 0 <= m < NBLK // 4:
                    sum_batch(m)
                for kind, p, *at in AT.get(slot, []):
                    if kind == "project":
                        project(p)
                    elif kind == "project_bc":
                        project_bc(p, at[0])
                    elif kind == "project_dt":
                        project_dt(p)
                    elif kind == "turn_y":
                        turn_y(p)
                    elif kind == "turn_x":
                        turn_x(p)
                    elif kind == "route":
                        route(p)
                    elif kind == "turn_w":
                        turn_w(p)
                    elif kind == "gate":
                        gate_or_up(p, at[0], "gate")
                    elif kind == "up":
                        gate_or_up(p, at[0], "up")
                    elif kind == "weight":
                        weight(p, at[0])
                    elif kind == "down":
                        down(p, *at)
                if 0 <= slot + 2 < NBLK:
                    u_block(slot + 2)

        @block.scalar
        def _(act):
            steps = [0]

            def then(ins):
                steps[0] += 1
                ins.then_inc(act_step, 1)
                act.wait_ge(act_step, steps[0])

            def pad(p):
                if p == 0:
                    act.wait_ge(zeroed, 1)
                for h in range(HV):
                    ps = full(act, ("project", p, h))
                    if p >= 1:
                        act.wait_ge(tapped, DC * HV * p)
                    ins = nc.scalar.activation(xpad[:, h, :, DC - 1:], ps[:].rearrange("p (b l) -> p b l", b=NB),
                                               ACT.Copy)
                    free(ins, ("project", p, h))

            def conv_silu(p):
                lay = p // NCH
                if p >= 2:
                    act.wait_ge(y_summed, 8 * (p - 2) + 5)
                for h in range(HV):
                    act.wait_ge(tapped, DC * HV * p + HV * (DC - 1) + h + 1)
                    nc.scalar.activation(u[:, p % 2, h, :], conv[:, h].rearrange("p b l -> p (b l)"), ACT.Silu,
                                         bias=chan[:, lay, h, 4:5]).then_inc(u_ready, 1)

            def keep_bc(p, i):
                if p >= 2 and i == 0:
                    act.wait_ge(weighted, BP * (p - 1))
                if p >= 2 and i == 1:
                    act.wait_ge(c_weighted, BP * (p - 1))
                ps = full(act, ("project_bc", p, i))
                dst = (brep[:, p % 2, :], crep[:, p % 2, :], dtlo[:])[i]
                free(nc.scalar.activation(dst, ps[:] if i < 2 else ps[0:DR, :], ACT.Copy), ("project_bc", p, i))

            def dt_bias(p):
                if p >= 1:
                    act.wait_ge(delta_ready, 2 * p)
                for h in range(HV):
                    ps = full(act, ("project_dt", p, h))
                    free(nc.scalar.activation(dtv[:, h * CH:(h + 1) * CH], ps[:], ACT.Identity,
                                              bias=chan[:, p // NCH, h, 5:6]), ("project_dt", p, h))

            def dt_abs(p):
                for h in range(HV):
                    wait_read(act, ("project_dt", p, h))
                if p >= 1:
                    act.wait_ge(lost_ready, 2 * p)
                nc.scalar.activation(dtt[:], dtv, ACT.Abs).then_inc(abs_ready, 1)

            def dt_exp(p):
                act.wait_ge(abs_ready, p + 1)
                nc.scalar.activation(dtt[:], dtt[:], ACT.Exp, scale=-1.0).then_inc(exp_ready, 1)

            def dt_ln(p):
                act.wait_ge(exp_ready, p + 1)
                if p >= 1:
                    act.wait_ge(log_summed, 2 * p)
                nc.scalar.activation(dtl[:], dtt[:], ACT.Ln, bias=1.0).then_inc(ln_ready, 1)

            def hi(p, q, h):
                if q == 0:
                    act.wait_ge(delta_ready, 2 * p + h + 1)
                else:
                    act.wait_ge(delta_u_ready, 2 * p + h + 1)
                if p >= 1:
                    act.wait_ge(stacked[h], 16 * 4 * NPART * p)
                nc.scalar.activation(parts[:, 0, q, h, :], val[:, q, h, :], ACT.Copy).then_inc(hi_ready, 1)

            def mid(p, q, h):
                act.wait_ge(rest_ready, order(p, q, h))
                nc.scalar.activation(parts[:, 1, q, h, :], val[:, q, h, :], ACT.Copy).then_inc(mid_ready, 1)

            def decay(k):
                p, b = divmod(k, BP)
                if k == 0:
                    act.wait_ge(a_made, 1)
                    act.wait_ge(zeroed, 2)
                if k >= NDA:
                    act.wait_ge(scanned, k - NDA + 1)
                act.wait_ge(delta_spread, k + 1)
                nc.scalar.activation(da[:, k % NDA, :, 1:], dps[k % 2][:].rearrange("p (b l) -> p b l", b=NB)[:, :, 1:],
                                     ACT.Exp, scale=aneg[:, p // NCH, b:b + 1]).then_inc(decayed, 1)

            def gate_silu(p):
                act.wait_ge(gate_shift, p + 1)
                if p >= 1:
                    full(act, ("turn_y", p - 1, 1))
                for t in range(TT):
                    b, h = divmod(t, HV)
                    nc.scalar.activation(sz[:, h, b * L:(b + 1) * L], xs[:, TT * (p % NCH) + t, :], ACT.Silu,
                                         bias=shift[:, t:t + 1], scale=rstd[0][:, t:t + 1]).then_inc(gate_ready, 1)

            def keep_xt(p):
                for k in range(KX):
                    ps = full(act, ("turn_x", p, k))
                    ins = nc.scalar.activation(xnt[:, k, :], ps[:], ACT.Copy)
                    free(ins, ("turn_x", p, k))

            def tanh(p, t):
                n = first_tile(p) + t
                ps = full(act, ("gate", p, t))
                if n >= 2:
                    wait_read(act, tile_use("up", n - 2))
                nc.scalar.activation(th[:, n % 2, :], ps[:], ACT.Tanh, scale=0.5).then_inc(tanh_ready, 1)

            act.wait_ge(in_sel, 16 * NIN["sel"])
            nc.scalar.activation(aneg[:], alog[:], ACT.Exp).then_inc(a_exp, 1)
            for slot in SLOTS:
                if 0 <= slot + LEAD < NBLK:
                    decay(slot + LEAD)
                for kind, p, *at in AT.get(slot, []):
                    if kind == "pad":
                        pad(p)
                    elif kind == "conv_silu":
                        conv_silu(p)
                    elif kind == "keep_bc":
                        keep_bc(p, at[0])
                    elif kind == "dt_bias":
                        dt_bias(p)
                    elif kind == "dt_abs":
                        dt_abs(p)
                    elif kind == "dt_exp":
                        dt_exp(p)
                    elif kind == "dt_ln":
                        dt_ln(p)
                    elif kind == "hi":
                        hi(p, *at)
                    elif kind == "mid":
                        mid(p, *at)
                    elif kind == "gate_silu":
                        gate_silu(p)
                    elif kind == "keep_xt":
                        keep_xt(p)
                    elif kind == "tanh":
                        tanh(p, at[0])
                    elif kind == "route_exp":
                        act.wait_ge(routed, p - NCH + 1)
                        nc.scalar.activation(e21[:], d21[:], ACT.Exp).then_inc(route_expd, 1)
                    elif kind == "keep_w":
                        ps = full(act, ("turn_w", p))
                        ins = nc.scalar.activation(wts[:], ps[0:NPART * NE, :], ACT.Copy)
                        free(ins, ("turn_w", p))

        @block.vector
        def _(dve):
            steps = [0]

            def then(ins):
                steps[0] += 1
                ins.then_inc(dve_step, 1)
                dve.wait_ge(dve_step, steps[0])

            def tap(p, k):
                for h in range(HV):
                    w = chan[:, p // NCH, h, k:k + 1]
                    if k == 0:
                        wait_read(dve, ("project", p, h))
                        if p >= 1:
                            dve.wait_ge(delta_ready, 2 * (p - 1) + h + 1)
                        ins = nc.vector.tensor_scalar(conv[:, h], xpad[:, h, :, 0:L], w, None, ALU.mult)
                    else:
                        dve.wait_ge(tapped, DC * HV * p + HV * (k - 1) + h + 1)
                        ins = nc.vector.scalar_tensor_tensor(out=conv[:, h], in0=xpad[:, h, :, k:k + L], scalar=w,
                                                             in1=conv[:, h], op0=ALU.mult, op1=ALU.add)
                    ins.then_inc(tapped, 1)

            def round_up(p):
                dve.wait_ge(exp_ready, p + 1)
                if p >= 1:
                    dve.wait_ge(delta_ready, 2 * p)
                nc.vector.tensor_scalar(dta[:], dtt[:], 1.0, -1.0, ALU.add, ALU.add).then_inc(rounded, 1)

            def delta(p, h):
                dve.wait_ge(log_summed, 2 * p + h + 1)
                if p >= 1:
                    dve.wait_ge(lo_ready, order(p - 1, 0, h))
                nc.vector.scalar_tensor_tensor(out=val[:, 0, h, :], in0=dtv[:, h * CH:(h + 1) * CH], scalar=0.0,
                                               in1=dta[:, h * CH:(h + 1) * CH], op0=ALU.max, op1=ALU.add)\
                    .then_inc(delta_ready, 1)

            def times_b(k):
                p = k // BP
                dve.wait_ge(u_spread, k + 1)
                if k % BP == 0:
                    wait_read(dve, ("project_bc", p, 0))
                nc.vector.tensor_tensor(ups[k % 2][:], ups[k % 2][:], brep[:, p % 2, :], ALU.mult)\
                    .then_inc(weighted, 1)

            def scan(k):
                dve.wait_ge(decayed, k + 1)
                dve.wait_ge(weighted, k + 1)
                if k >= NHB:
                    dve.wait_ge(y_summed, (k - NHB) // 4 + 1)
                nc.vector.tensor_tensor_scan(hst[:, k % NHB, :], da[:, k % NDA].rearrange("p b l -> p (b l)"),
                                             ups[k % 2][:], 0.0, ALU.mult, ALU.add).then_inc(scanned, 1)

            def gate_y(half):
                p, h = divmod(half, HV)
                dve.wait_ge(y_summed, 4 * half + 4)
                dve.wait_ge(gate_ready, TT * (p + 1))
                nc.vector.tensor_tensor(sz[:, h, :], yps[:], sz[:, h, :], ALU.mult).then_inc(y_gated, 1)

            def stats(which, c):
                for i in range(TT):
                    nc.vector.bn_stats(bns[which][:, i, :], xs[:, TT * c + i, :]).then_inc(stats_made[which], 1)

            def aggregate(which, n):
                for i in range(TT):
                    dve.wait_ge(stats_made[which], TT * n + i + 1)
                    nc.vector.bn_aggr(mv[which][:, i, :], bns[which][:, i, :]).then_inc(aggregated[which], 1)
                dve.wait_ge(aggregated[which], TT * (n + 1))
                nc.vector.tensor_scalar(ve[which][:], mv[which][:, :, 1], EPS, None, ALU.add)\
                    .then_inc(var_ready[which], 1)

            def gate_stats(p):
                if p == 0:
                    dve.wait_ge(in_x, 16 * NIN["x"])
                if p >= NCH:
                    for i in range(2):
                        wait_read(dve, ("down", p - NCH, i))
                stats(0, p % NCH)

            def gate_shift_of(p):
                dve.wait_ge(rstd_ready[0], p + 1)
                if p >= 1:
                    dve.wait_ge(gate_ready, TT * p)
                nc.vector.scalar_tensor_tensor(out=shift[:], in0=mv[0][:, :, 0], scalar=-1.0, in1=rstd[0][:],
                                               op0=ALU.mult, op1=ALU.mult).then_inc(gate_shift, 1)

            def add_y(p):
                c = p % NCH
                for i in range(2):
                    ps = full(dve, ("turn_y", p, i))
                    t = TT * c + 2 * i
                    rows = xs[:, t:t + 2, :].rearrange("p a b -> p (a b)")
                    dve.wait_ge(gate_ready, TT * (p + 1))
                    ins = nc.vector.tensor_tensor(rows, ps[:], rows, ALU.add)
                    free(ins, ("turn_y", p, i))

            def ffn_stats(p):
                for i in range(2):
                    wait_read(dve, ("turn_y", p, i))
                stats(1, p % NCH)

            def ffn_norm(p):
                c = p % NCH
                dve.wait_ge(rstd_ready[1], p + 1)
                for t in range(TT):
                    ins = nc.vector.tensor_scalar(xn[:, t, :], xs[:, TT * c + t, :], mv[1][:, t, 0:1],
                                                  rstd[1][:, t:t + 1], ALU.subtract, ALU.mult)
                ins.then_inc(ffn_normed, 1)

            def silu(p, t):
                n = first_tile(p) + t
                dve.wait_ge(tanh_ready, n + 1)
                ps = full(dve, ("gate", p, t))
                ins = nc.vector.scalar_tensor_tensor(out=th[:, n % 2, :], in0=th[:, n % 2, :], scalar=1.0, in1=ps[:],
                                                     op0=ALU.add, op1=ALU.mult)
                free(ins, ("gate", p, t))

            def hidden(p, t):
                n = first_tile(p) + t
                wait_read(dve, ("gate", p, t))
                ps = full(dve, ("up", p, t))
                ins = nc.vector.scalar_tensor_tensor(out=hid[:, t, :], in0=th[:, n % 2, :], scalar=0.5, in1=ps[:],
                                                     op0=ALU.mult, op1=ALU.mult)
                free(ins, ("up", p, t))

            def weigh(p, t):
                wait_read(dve, ("up", p, t))
                ps = full(dve, ("weight", p, t))
                free(nc.vector.tensor_tensor(hid[:, t, :], ps[:], hid[:, t, :], ALU.mult), ("weight", p, t))

            def add_down(p, i):
                ps = full(dve, ("down", p, i))
                t = TT * (p % NCH) + 2 * i
                rows = xs[:, t:t + 2, :].rearrange("p a b -> p (a b)")
                ins = nc.vector.tensor_tensor(rows, ps[:], rows, ALU.add)
                free(ins, ("down", p, i))

            def top2(p):
                ps = full(dve, ("route", p))
                ins = nc.vector.tensor_copy(lg[:].rearrange("p t e -> p (t e)"), ps[:, 0:TT * NE])
                free(ins, ("route", p))
                wait_read(dve, ("route", p))
                for t in range(TT):
                    ins = nc.vector.max(top[:, t, :], lg[:, t, :])
                then(ins)
                for t in range(TT):
                    ins = nc.vector.max_index(tix[:, t, :], top[:, t, :], lg[:, t, :])
                then(ins)
                then(nc.vector.tensor_copy(tif[:], tix[:, :, 0:2]))
                nc.vector.tensor_tensor(d21[:], top[:, :, 1], top[:, :, 0], ALU.subtract).then_inc(routed, 1)

            def route_weights(p):
                dve.wait_ge(route_expd, p - NCH + 1)
                then(nc.vector.tensor_scalar(s21[:], e21[:], 1.0, None, ALU.add))
                then(nc.vector.reciprocal(p1[:], s21[:]))
                then(nc.vector.tensor_tensor(p2[:], e21[:], p1[:], ALU.mult))
                for t in range(TT):
                    nc.vector.tensor_scalar(m1[:, t, :], sml[:, 0:NE], tif[:, t, 0:1], p1[:, t:t + 1],
                                            ALU.is_equal, ALU.mult)
                    ins = nc.vector.tensor_scalar(m2[:, t, :], sml[:, 0:NE], tif[:, t, 1:2], p2[:, t:t + 1],
                                                  ALU.is_equal, ALU.mult)
                then(ins)
                then(nc.vector.tensor_tensor(wtok[:], m1[:], m2[:], ALU.add))
                left = wtok[:]
                for k in range(NPART):
                    then(nc.vector.tensor_copy(whb[:, :, k, :], left))
                    if k < NPART - 1:
                        then(nc.vector.tensor_tensor(wr[:, :, k, :], left, whb[:, :, k, :], ALU.subtract))
                        left = wr[:, :, k, :]
                nc.vector.tensor_copy(wprt[:], whb[:]).then_inc(weights_made, 1)

            nc.vector.memset(xpad[:, :, :, 0:DC - 1], 0.0).then_inc(zeroed, 1)
            nc.vector.memset(da[:, :, :, 0:1], 0.0).then_inc(zeroed, 1)
            dve.wait_ge(in_ctx, 16 * NIN["ctx"])
            for lay in range(2):
                for h in range(HV):
                    for i in range(2):
                        cols = xpr[:, lay, h, DR + i * DS:DR + (i + 1) * DS]
                        ins = nc.vector.tensor_copy(xbc[:, lay, h, i],
                                                    cols.unsqueeze(1).to_broadcast([P, EB, DS]))
            ins.then_inc(consts_made, 1)
            dve.wait_ge(in_sel, 16 * NIN["sel"])
            nc.vector.tensor_copy(sels[:], sels32)
            for lay in range(2):
                for h in range(HV):
                    ins = nc.vector.tensor_scalar(dperm[:, lay, h, :], prm[:], chan[:, lay, h, 6:7], None, ALU.mult)
            ins.then_inc(consts_made, 1)
            dve.wait_ge(a_exp, 1)
            nc.vector.tensor_scalar(aneg[:], aneg[:], -1.0, None, ALU.mult).then_inc(a_made, 1)
            for slot in SLOTS:
                if 0 <= slot < NBLK:
                    scan(slot)
                if 0 <= slot + 1 < NBLK:
                    times_b(slot + 1)
                half, r = divmod(slot - BH - 4, BH)
                if r == 0 and 0 <= half < NBLK // BH:
                    gate_y(half)
                if slot == 0:
                    dve.wait_ge(in_moe, 16 * NIN["moe"])
                    nc.vector.tensor_copy(selw[:], selw32).then_inc(consts_made, 1)
                for kind, p, *at in AT.get(slot, []):
                    if kind == "tap":
                        tap(p, at[0])
                    elif kind == "round_up":
                        round_up(p)
                    elif kind == "delta":
                        delta(p, at[0])
                    elif kind == "gate_stats":
                        gate_stats(p)
                    elif kind == "gate_aggr":
                        aggregate(0, p)
                    elif kind == "ffn_stats":
                        ffn_stats(p)
                    elif kind == "ffn_aggr":
                        aggregate(1, p)
                    elif kind == "gate_shift":
                        gate_shift_of(p)
                    elif kind == "add_y":
                        add_y(p)
                    elif kind == "ffn_norm":
                        ffn_norm(p)
                    elif kind == "top2":
                        top2(p)
                    elif kind == "route_w":
                        route_weights(p)
                    elif kind == "silu":
                        silu(p, at[0])
                    elif kind == "hidden":
                        hidden(p, at[0])
                    elif kind == "weigh":
                        weigh(p, at[0])
                    elif kind == "add_down":
                        add_down(p, at[0])

        @block.gpsimd
        def _(pool):
            def times_c(k):
                p = k // BP
                pool.wait_ge(scanned, k + 1)
                if k % BP == 0:
                    wait_read(pool, ("project_bc", p, 1))
                nc.gpsimd.tensor_tensor(hst[:, k % NHB, :], hst[:, k % NHB, :], crep[:, p % 2, :], ALU.mult)\
                    .then_inc(c_weighted, 1)

            def power(which, n):
                pool.wait_ge(var_ready[which], n + 1)
                if n == 0 and which == 0:
                    pool.wait_ge(in_moe, 16 * NIN["moe"])
                nc.gpsimd.tensor_tensor(rstd[which][:], ve[which][:], sml[:, NE:NE + TT], ALU.pow)\
                    .then_inc(rstd_ready[which], 1)

            def lost(p, h):
                pool.wait_ge(rounded, p + 1)
                part = slice(h * CH, (h + 1) * CH)
                nc.gpsimd.tensor_tensor(dta[:, part], dtt[:, part], dta[:, part], ALU.subtract).then_inc(lost_ready, 1)

            def log_sum(p, h):
                pool.wait_ge(ln_ready, p + 1)
                pool.wait_ge(lost_ready, 2 * p + h + 1)
                part = slice(h * CH, (h + 1) * CH)
                nc.gpsimd.tensor_tensor(dta[:, part], dta[:, part], dtl[:, part], ALU.add).then_inc(log_summed, 1)

            def delta_u(p, h):
                pool.wait_ge(delta_ready, 2 * p + h + 1)
                pool.wait_ge(u_ready, 2 * p + h + 1)
                if p >= 1:
                    pool.wait_ge(lo_ready, order(p - 1, 1, h))
                nc.gpsimd.tensor_tensor(val[:, 1, h, :], val[:, 0, h, :], u[:, p % 2, h, :], ALU.mult)\
                    .then_inc(delta_u_ready, 1)

            def rest(p, q, h):
                pool.wait_ge(hi_ready, order(p, q, h))
                if q == 0:
                    pool.wait_ge(delta_u_ready, 2 * p + h + 1)
                nc.gpsimd.tensor_tensor(val[:, q, h, :], val[:, q, h, :], parts[:, 0, q, h, :], ALU.subtract)\
                    .then_inc(rest_ready, 1)

            def lo(p, q, h):
                pool.wait_ge(mid_ready, order(p, q, h))
                nc.gpsimd.tensor_tensor(parts[:, 2, q, h, :], val[:, q, h, :], parts[:, 1, q, h, :], ALU.subtract)\
                    .then_inc(lo_ready, 1)

            for slot in SLOTS:
                if 0 <= slot < NBLK:
                    times_c(slot)
                for kind, p, *at in AT.get(slot, []):
                    if kind == "gate_rstd":
                        power(0, p)
                    elif kind == "ffn_rstd":
                        power(1, p)
                    elif kind == "lost":
                        lost(p, at[0])
                    elif kind == "log_sum":
                        log_sum(p, at[0])
                    elif kind == "delta_u":
                        delta_u(p, at[0])
                    elif kind == "rest":
                        rest(p, *at)
                    elif kind == "lo":
                        lo(p, *at)


def kernel(**inputs):
    import concourse.bacc as bacc
    from concourse.bass_utils import run_bass_kernel_spmd

    a = {k: np.ascontiguousarray(v) for k, v in inputs.items()}
    f = np.float32
    q = np.arange(P)
    chan_of_q = 32 * (q // 8 % 4) + 8 * (q // 32) + q % 8
    order = np.concatenate([h * P + chan_of_q for h in range(HV)])
    layers = ("L0_xattn_", "L1_xattn_")

    def stacked(name, lay_out):
        return np.stack([lay_out(a[n + name]) for n in layers])

    def rows(w):
        return w[order].reshape(HV, P, -1).transpose(1, 0, 2)

    def k_tiles(w):
        return w.reshape(-1, P, w.shape[-1]).transpose(1, 0, 2)

    def by_block(w):
        return w[order].reshape(HV * BH, EB * DS).T

    arrays = {
        "x": k_tiles(a["x"].reshape(TOK, DX)),
        "ctx_t": a["ctx_1024"].reshape(TOK, DM).T,
        "in_proj_t": stacked("in_proj_w", lambda w: w[order].reshape(HV, P, DM).transpose(2, 0, 1)).transpose(1, 0, 2, 3),
        "channel": np.stack([np.concatenate(
            [rows(a[n + "conv_w"].reshape(DI, DC))] + [rows(a[n + m].reshape(DI, 1)) for m in ("conv_b", "dt_proj_b", "D")],
            axis=-1) for n in layers], axis=1),
        "x_proj_t": stacked("x_proj_w", lambda w: rows(w.T)).transpose(1, 0, 2, 3),
        "dt_proj_t": stacked("dt_proj_w", lambda w: w[order].reshape(HV, P, DR).transpose(2, 0, 1)).transpose(1, 0, 2, 3),
        "a_log": stacked("A_log", by_block).transpose(1, 0, 2),
        "w_gate_t": k_tiles(a["L0_ffn_w_gate"].T),
        "w_up_t": k_tiles(a["L0_ffn_w_up"].T),
        "w_down_t": k_tiles(a["L0_ffn_w_down"].T),
        "route_w": k_tiles(a["L1_ffn_gate_w"]),
        "w1_t": k_tiles(a["L1_ffn_w1"].transpose(1, 0, 2).reshape(DX, MOE)),
        "w3_t": k_tiles(a["L1_ffn_w3"].transpose(1, 0, 2).reshape(DX, MOE)),
        "w2_t": k_tiles(a["L1_ffn_w2"].reshape(MOE, DX)),
    }
    r = np.arange(NPART * 32)
    arrays["sel_spread"] = np.stack([(r[:, None] % 32 == EB * j + q[None, :] // DS) for j in range(4)], 1).astype(f)
    arrays["sel_sum"] = np.stack([(EB * s + q[:, None] // DS == np.arange(32)[None, :]) for s in range(4)], 1).astype(f)
    arrays["perm"] = (chan_of_q[:, None] == q[None, :]).astype(f)
    arrays["ident"] = np.eye(P, dtype=f)
    arrays["sel_weight"] = (np.arange(NPART * NE)[:, None] % NE == np.arange(MOE)[None, :] // EI).astype(f)
    arrays["small"] = np.concatenate([np.tile(np.arange(NE, dtype=f), (P, 1)), np.full((P, TT), -0.5, f)], axis=1)

    nc = bacc.Bacc("TRN2", target_bir_lowering=False, num_devices=1)
    arrays = {k: np.ascontiguousarray(v) for k, v in arrays.items()}
    args = [nc.dram_tensor(k, v.shape, mybir.dt.float32, kind="ExternalInput").ap() for k, v in arrays.items()]
    out = nc.dram_tensor("out", (P, TOK // P, DX), mybir.dt.float32, kind="ExternalOutput").ap()
    build(nc, *args, out)
    got = run_bass_kernel_spmd(nc, [arrays], core_ids=[0]).results[0]["out"]
    return np.ascontiguousarray(got.transpose(1, 0, 2)).reshape(B, L, DX)
```

```python
import numpy as np
import concourse.bass as bass
from concourse import mybir
from contextlib import ExitStack

P = 128
B, L, DX = 4, 256, 256
TOK = B * L
CH = 512
NB = CH // L
NCH = TOK // CH
TT = CH // P
DM, DI, DS, DR, DC = 128, 256, 16, 8, 4
HV = DI // P
EB = P // DS
BH = P // EB
BP = HV * BH
NPASS = 2 * NCH
NBLK = NPASS * BP
KX = DX // P
HID = 1024
NE, EI = 8, 176
MOE = NE * EI
EPS = 1e-5
NPART = 3
PADW = DC - 1 + L

LEAD = 2
NDA, NHB = 5, 9
SUMLAG = 7


def tiles_of(p):
    return HID // P if p < NCH else MOE // P


def first_tile(p):
    return sum(tiles_of(i) for i in range(p))


def on_vector(p, h):
    return (p, h) in VPARTS


def weigh_on_pool(p):
    return p == NCH


def hidden_on_pool(p, t):
    return t in HIDDEN_ON_POOL[p]


STEP = dict(
    spread_taps=(-5, -32, None, None), scale_taps=(-4, -29, None, None), conv00=(-5, -26, -30, -51),
    conv01=(-2, -25, -26, -46), conv_silu0=(-1, -22, -23, -45), conv10=(-5, -24, -24, -48),
    conv11=(-4, -22, -23, -47), conv_silu1=(-1, -22, -23, -45), project_x=(-2, -1, 1, -3),
    keep_x=(0, 1, 0, 1), project_dt=(3, 4, 5, 4), dt_bias=(4, 6, 5, 5), dt_abs=(10, 7, 8, 6),
    dt_exp=(10, 8, 9, 10), dt_ln=(10, 9, 12, 10), round_up=(12, 11, 11, 11), lost0=(13, 12, 11, 10),
    log_sum0=(17, 13, 12, 11), delta0=(18, 15, 14, 14), delta_u0=(21, 15, 13, 17), lost1=(17, 14, 14, 9),
    log_sum1=(23, 16, 17, 17), delta1=(22, 18, 18, 18), delta_u1=(23, 20, 20, 18), hi00=(13, 17, 15, 15),
    rest00=(21, 17, 17, 19), mid00=(23, 17, 19, 19), lo00=(25, 18, 18, 22), hi10=(23, 17, 18, 17),
    rest10=(22, 19, 19, 19), mid10=(26, 22, 20, 22), lo10=(26, 22, 23, 25), hi01=(24, 20, 19, 21),
    rest01=(27, 24, 20, 20), mid01=(26, 24, 21, 21), lo01=(31, 26, 24, 22), hi11=(26, 25, 22, 21),
    rest11=(28, 26, 22, 22), mid11=(33, 28, 27, 27), lo11=(33, 27, 24, 26),
    gate_stats=(8, 14, 13, 14), gate_aggr=(9, 16, 14, 14), gate_rstd=(8, 15, 13, 13),
    gate_shift=(12, 17, 18, 15), gate_silu=(13, 17, 19, 19),
    turn_y=(6, 6, 6, 7), add_y=(6, 6, 6, 7), ffn_stats=(6, 7, 7, 7), ffn_aggr=(7, 8, 7, 7),
    ffn_rstd=(7, 8, 6, 7), ffn_norm=(8, 9, 10, 9), turn_x=(9, 13, 12, 13), keep_xt=(11, 12, 12, 11),
    net=(14, 14, 14, 15), route=(None, None, 15, 17), top2=(None, None, 16, 14),
    route_exp=(None, None, 16, 14), route_w=(None, None, 18, 21), turn_w=(None, None, 21, 26),
    keep_w=(None, None, 23, 27), weight=(None, None, 26, 31),
    tanh=(0, 0, 0, 2), silu=(1, 1, 1, 4), keep_up=(1, 1, 1, 0), hidden=(1, 1, 1, 4),
    keep_weight=(None, None, 0, None), weigh=(None, None, 1, 3), add_down=(1, 1, 1, 4),
)
HIDDEN_ON_POOL = ({3, 4, 5, 6}, {4, 7}, {0, 1, 2, 3, 6, 7, 9}, set())
VPARTS = {(0, 0), (1, 0)}
CONSTS = -35
SKIP = {44, 45, 54, 56, 57, 60, 63, 65, 68, 88, 95, 99, 100, 102, 106, 132, 134, 135, 138, 141, 144, 146, 147,
        148, 158, 159, 162, 163, 168}
PAIRS = {44, 52, 133, 136, 143, 154}


def schedule():
    at = {}

    def put(slot, *step):
        at.setdefault(slot, []).append(step)

    for p in range(NPASS):
        def off(name):
            return STEP[name][p]

        def step(stage, name, *which, key=""):
            put(BP * stage + off(name + key), name, p, *which)

        if p < 2:
            step(p - 1, "spread_taps")
            step(p - 1, "scale_taps")
        for h in range(HV):
            for half in range(2):
                step(p - 1, "conv", h, half, key=f"{h}{half}")
            step(p - 1, "conv_silu", h, key=str(h))
        for name in ("project_x", "keep_x", "project_dt", "dt_bias", "dt_abs", "dt_exp", "dt_ln",
                     "round_up"):
            step(p - 1, name)
        for h in range(HV):
            for name in ("lost", "log_sum", "delta", "delta_u"):
                step(p - 1, name, h, key=str(h))
        for q, h in ((0, 0), (1, 0), (0, 1), (1, 1)):
            for name in ("hi", "rest", "mid", "lo"):
                step(p - 1, name, q, h, key=f"{q}{h}")
        for name in ("gate_stats", "gate_aggr", "gate_rstd", "gate_shift", "gate_silu"):
            step(p, name)
        for name in ("turn_y", "add_y", "ffn_stats", "ffn_aggr", "ffn_rstd", "ffn_norm", "turn_x", "keep_xt"):
            step(p + 1, name)
        s = BP * (p + 1)
        n, moe = tiles_of(p), p >= NCH
        free = (k for k in range(s + off("net"), s + 150) for _ in range((k not in SKIP) + (k in PAIRS)))
        for t in range(n):
            k = next(free)
            put(k, "gate", p, t)
            put(k + off("tanh"), "tanh", p, t)
            put(k + off("silu"), "silu", p, t)
            k = next(free)
            put(k, "up", p, t)
            if hidden_on_pool(p, t):
                put(k + off("keep_up"), "keep_up", p, t)
            put(k + off("hidden"), "hidden", p, t)
            if (p, t) == (NCH - 1, n - 1):
                put(k, "fetch", p, 0)
                put(k + 1, "fetch", p, 1)
            if moe:
                j = max(s + off("weight") + t, k + 2)
                put(j, "weight", p, t)
                if weigh_on_pool(p):
                    put(j + off("keep_weight"), "keep_weight", p, t)
                put(j + off("weigh"), "weigh", p, t)
                if t == n - 1:
                    next(free), next(free)
            elif t == n - 1:
                next(free)
        if moe:
            for name in ("route", "top2", "route_exp", "route_w", "turn_w", "keep_w"):
                step(p + 1, name)
        for t in range(TT):
            for part in range(2):
                k = next(free)
                put(k, "down", p, t, part)
            if t % 2:
                put(k + off("add_down"), "add_down", p, t // 2)
        if p == NCH - 1:
            put(k + 1, "fetch", p, 2)
    return at


AT = schedule()
SLOTS = range(min(AT), max(AT) + 1)


READER = {"spread_taps": "scale_taps", "conv": "conv_silu", "project_x": "keep_x", "project_dt": "dt_bias",
          "turn_y": "add_y", "turn_x": "keep_xt", "route": "top2", "turn_w": "keep_w", "gate": "silu", "up": "hidden",
          "weight": "weigh", "down": "add_down"}


def bank_uses():
    slot_of = {step: slot for slot, steps in AT.items() for step in steps}
    uses, read, count = {}, [min(AT)] * 3, [0] * 7
    for slot in SLOTS:
        if slot == NBLK + 1:
            read += [NBLK - 1] * 4
        for kind, p, *at in AT.get(slot, []):
            if kind not in READER or (kind == "down" and (at[0] % 2 or at[1])) or (kind == "conv" and at[1]):
                continue
            pair = kind in ("spread_taps", "project_dt", "turn_y", "turn_x")
            for i in range(2) if pair else (at[0] // 2,) if kind == "down" else at[:1] or (None,):
                use = (kind, p) if i is None else (kind, p, i)
                reader = ("keep_weight" if kind == "weight" and weigh_on_pool(p) else
                          "keep_up" if kind == "up" and hidden_on_pool(p, at[0]) else READER[kind])
                b = read.index(min(read))
                uses[use] = (b, count[b])
                count[b] += 1
                read[b] = slot_of[(reader, p) if pair else (reader,) + use[1:]]
    return uses


USE = bank_uses()


def build(nc, x, ctx_t, in_proj_t, conv_w, channel, x_proj_t, dt_proj_t, a_log, w_gate_t, w_up_t, w_down_t,
          route_w, w1_t, w3_t, w2_t, sel_spread, sel_sum, perm, ident, sel_weight, small, out):
    f32, bf16, u32 = mybir.dt.float32, mybir.dt.bfloat16, mybir.dt.uint32
    ALU, ACT = mybir.AluOpType, mybir.ActivationFunctionType
    ctx = ExitStack()
    with ctx:
        def sb(name, shape, dt=f32):
            return ctx.enter_context(nc.sbuf_tensor(name, shape, dt))

        def sem(name):
            return ctx.enter_context(nc.semaphore(name))

        xs = sb("xs", [P, TOK // P, DX])
        ctxt = sb("ctxt", [P, B, PADW])
        chan = sb("chan", [P, 2, HV, 3])
        xpr = sb("xpr", [P, 2, HV, DR + 2 * DS])
        dtp = sb("dtp", [DR, 2, HV, P])
        alog = sb("alog", [P, 2, BP])
        wa, wb, wc = sb("wa", [P, KX * MOE]), sb("wb", [P, KX * MOE]), sb("wc", [P, MOE // P, DX])
        wg, wu = (w[:, 0:KX * HID].rearrange("p (k n) -> p k n", k=KX) for w in (wa, wb))
        w1, w3 = (w[:].rearrange("p (k n) -> p k n", k=KX) for w in (wa, wb))
        rw = sb("rw", [P, KX, NE])
        hid = sb("hid", [P, MOE // P, CH])
        wconv = hid[:, 5:5 + 2 * HV, :].rearrange("p a (k e) -> p a k e", k=DC)
        sels32 = hid[0:NPART * 32, 4, :].rearrange("p (j n) -> p j n", j=4)
        selw32 = hid[0:NPART * NE, 0:3, :].rearrange("p a n -> p (a n)")[:, 0:MOE]
        inp = hid[:, 9, :].rearrange("p (l h e) -> p l h e", l=2, h=HV)
        prm = hid[:, 10, 0:P]
        sely = sb("sely", [P, 4, 32])
        idn = sb("idn", [P, P])
        sml = sb("sml", [P, NE + TT])
        sels = sb("sels", [NPART * 32, 4, P], bf16)
        selw = sb("selw", [NPART * NE, MOE], bf16)
        aneg = sb("aneg", [P, 2, BP])
        dperm = sb("dperm", [P, 2, HV, P])
        ones = sb("ones", [1, P])
        u = sb("u", [P, NPASS, HV, CH])
        brep = sb("brep", [P, 2, CH])
        crep = sb("crep", [P, 2, CH])
        xdbl = sb("xdbl", [DR + 2 * DS, CH])
        dtv = sb("dtv", [P, HV * CH])
        dtt = sb("dtt", [P, HV * CH])
        dtl = sb("dtl", [P, HV * CH])
        dta = sb("dta", [P, HV * CH])
        val = sb("val", [P, 2, HV, CH])
        parts = sb("parts", [P, NPART, 2, HV, CH], bf16)
        stack = sb("stack", [NPART * 32, HV, 2, 4, CH], bf16)
        da = sb("da", [P, NDA, NB, L])
        hst = sb("hst", [P, NHB, CH])
        taps = hst[0:1, 0:2 * HV, :]
        sz = sb("sz", [P, HV, CH])
        bns = [sb(f"bns{i}", [P, TT, 6]) for i in range(2)]
        mv = [sb(f"mv{i}", [P, TT, 2]) for i in range(2)]
        ve = [sb(f"ve{i}", [P, TT]) for i in range(2)]
        rstd = [sb(f"rstd{i}", [P, TT]) for i in range(2)]
        shift = sb("shift", [P, TT])
        xn = sb("xn", [P, TT, DX])
        upc = xn[:].rearrange("p t d -> p (t d)").rearrange("p (i n) -> p i n", i=2)
        xnt = sb("xnt", [P, KX, CH])
        th = sb("th", [P, 2, CH])
        wgt = sb("wgt", [P, 2, CH])
        lg = sb("lg", [P, TT, NE])
        top = sb("top", [P, TT, NE])
        tix = sb("tix", [P, TT, NE], u32)
        tif = sb("tif", [P, TT, 2])
        d21 = sb("d21", [P, TT])
        e21 = sb("e21", [P, TT])
        s21 = sb("s21", [P, TT])
        p1 = sb("p1", [P, TT])
        p2 = sb("p2", [P, TT])
        m1 = sb("m1", [P, TT, NE])
        m2 = sb("m2", [P, TT, NE])
        wtok = sb("wtok", [P, TT, NE])
        whb = sb("whb", [P, TT, NPART, NE], bf16)
        wr = sb("wr", [P, TT, 2, NE])
        wprt = sb("wprt", [P, TT, NPART, NE])
        wts = sb("wts", [NPART * NE, CH], bf16)

        def bank(name):
            return ctx.enter_context(nc.psum_tensor(name, [P, CH], f32))

        dps = [bank(f"dps{i}") for i in range(2)]
        ups = [bank(f"ups{i}") for i in range(2)]
        yps = bank("yps")
        gen = [bank(f"gen{i}") for i in range(3)] + dps + ups

        in_ctx, in_sel, in_x, in_ffn, in_moe = (sem(n) for n in (
            "in_ctx", "in_sel", "in_x", "in_ffn", "in_moe"))
        in_w = [sem(f"in_{n}") for n in ("w1", "w3", "w2")]
        consts_made, a_exp, a_made = sem("consts_made"), sem("a_exp"), sem("a_made")
        zeroed = sem("zeroed")
        bank_full = [sem(f"bank_full{i}") for i in range(7)]
        bank_read = [sem(f"bank_read{i}") for i in range(7)]
        in_taps, in_proj = sem("in_taps"), sem("in_proj")
        b_spread, c_spread = ([sem(f"{n}{i}") for i in range(2)] for n in ("b_spread", "c_spread"))
        abs_ready, exp_ready, ln_ready, rounded = (sem(n) for n in (
            "abs_ready", "exp_ready", "ln_ready", "rounded"))
        lost_ready, log_summed, delta_ready, delta_u_ready, hi_ready, rest_ready, mid_ready, lo_ready = (
            [sem(f"{n}{h}") for h in range(HV)] for n in (
                "lost_ready", "log_summed", "delta_ready", "delta_u_ready",
                "hi_ready", "rest_ready", "mid_ready", "lo_ready"))
        stacked = [[sem(f"stacked{h}{s}") for s in range(4)] for h in range(HV)]
        delta_spread, decayed, u_spread, weighted, scanned, c_weighted, y_summed, y_gated = (sem(n) for n in (
            "delta_spread", "decayed", "u_spread", "weighted", "scanned", "c_weighted", "y_summed", "y_gated"))
        stats_made, aggregated, var_ready, rstd_ready = (
            [sem(f"{n}_{norm}") for norm in ("gate", "ffn")]
            for n in ("stats_made", "aggregated", "var_ready", "rstd_ready"))
        gate_shift, gate_ready, ffn_normed, tanh_ready = (sem(n) for n in (
            "gate_shift", "gate_ready", "ffn_normed", "tanh_ready"))
        routed, route_expd, weights_made = (sem(n) for n in ("routed", "route_expd", "weights_made"))
        weighed, pool_hidden = sem("weighed"), sem("pool_hidden")
        stored = sem("stored")
        dve_step = sem("dve_step")

        block = ctx.enter_context(nc.Block())
        NIN = {"ctx": 4, "sel": 4, "x": 1, "ffn": 3, "moe": 4}

        def full(eng, use):
            b, n = USE[use]
            eng.wait_ge(bank_full[b], n + 1)
            return gen[b]

        def free(ins, use):
            ins.then_inc(bank_read[USE[use][0]], 1)

        def wait_read(eng, use):
            b, n = USE[use]
            eng.wait_ge(bank_read[b], n + 1)

        def tile_use(kind, n):
            p = max(i for i in range(NPASS) if first_tile(i) <= n)
            return kind, p, n - first_tile(p)

        def pool_tiles(p, t):
            before = sum(len(HIDDEN_ON_POOL[i]) for i in range(p))
            return before + sum(t is None or i <= t for i in HIDDEN_ON_POOL[p])

        def wait_hidden(eng, p, t):
            if hidden_on_pool(p, t):
                eng.wait_ge(pool_hidden, pool_tiles(p, t))
            else:
                wait_read(eng, ("up", p, t))

        def wait_net(eng, p, t):
            if p >= 1 and t == min(j for j in range(tiles_of(p)) if hidden_on_pool(p, j) == hidden_on_pool(p, t)):
                full(eng, ("down", p - 1, 1))

        def order(p, q):
            return 2 * p + q + 1

        def spread_bc(sync, p):
            wait_read(sync, ("project_x", p))
            if p >= 2:
                sync.wait_ge(weighted, BP * (p - 1))
                sync.wait_ge(c_weighted, BP * (p - 1))
            for i, (rep, ready) in enumerate(((brep, b_spread), (crep, c_spread))):
                for c in range(EB):
                    sync.dma_start(rep[DS * c:DS * (c + 1), p % 2, :],
                                   xdbl[DR + DS * i:DR + DS * (i + 1), :]).then_inc(ready[p % 2], 16)

        def stack_parts(sync, p, h):
            sync.wait_ge(hi_ready[h], order(p, 1))
            sync.wait_ge(mid_ready[h], order(p, 1))
            sync.wait_ge(lo_ready[h], order(p, 1))
            for s in range(4):
                if p >= 1:
                    sync.wait_ge(delta_spread, BP * (p - 1) + BH * h + 4 * (s + 1))
                    sync.wait_ge(u_spread, BP * (p - 1) + BH * h + 4 * (s + 1))
                for k in range(NPART):
                    sync.dma_start(stack[32 * k:32 * k + 32, h, :, s, :],
                                   parts[32 * s:32 * s + 32, k, :, h, :]).then_inc(stacked[h][s], 16)

        def lost(eng, alu, p, h):
            eng.wait_ge(rounded, p + 1)
            part = slice(h * CH, (h + 1) * CH)
            alu.tensor_tensor(dta[:, part], dtt[:, part], dta[:, part], ALU.subtract).then_inc(lost_ready[h], 1)

        def log_sum(eng, alu, p, h):
            eng.wait_ge(ln_ready, p + 1)
            eng.wait_ge(lost_ready[h], p + 1)
            part = slice(h * CH, (h + 1) * CH)
            alu.tensor_tensor(dta[:, part], dta[:, part], dtl[:, part], ALU.add).then_inc(log_summed[h], 1)

        def delta_u(eng, alu, p, h):
            eng.wait_ge(delta_ready[h], p + 1)
            wait_read(eng, ("conv", p, h))
            if p >= 1:
                eng.wait_ge(lo_ready[h], order(p - 1, 1))
            alu.tensor_tensor(val[:, 1, h, :], val[:, 0, h, :], u[:, p, h, :], ALU.mult)\
                .then_inc(delta_u_ready[h], 1)

        def rest(eng, alu, p, q, h):
            eng.wait_ge(hi_ready[h], order(p, q))
            if q == 0:
                eng.wait_ge(delta_u_ready[h], p + 1)
            alu.tensor_tensor(val[:, q, h, :], val[:, q, h, :], parts[:, 0, q, h, :], ALU.subtract)\
                .then_inc(rest_ready[h], 1)

        def lo(eng, alu, p, q, h):
            eng.wait_ge(mid_ready[h], order(p, q))
            alu.tensor_tensor(parts[:, 2, q, h, :], val[:, q, h, :], parts[:, 1, q, h, :], ALU.subtract)\
                .then_inc(lo_ready[h], 1)

        @block.sync
        def _(sync):
            sync.dma_start(taps, conv_w).then_inc(in_taps, 16)
            sync.dma_start(inp, in_proj_t).then_inc(in_proj, 16)
            sync.dma_start(ctxt[:, :, DC - 1:], ctx_t.rearrange("p (b l) -> p b l", b=B)).then_inc(in_ctx, 16)
            sync.dma_start(chan[:], channel).then_inc(in_ctx, 16)
            sync.dma_start(xpr[:], x_proj_t).then_inc(in_ctx, 16)
            sync.dma_start(dtp[:], dt_proj_t).then_inc(in_ctx, 16)
            sync.dma_start(alog[:], a_log).then_inc(in_sel, 16)
            sync.dma_start(sels32, sel_spread).then_inc(in_sel, 16)
            sync.dma_start(sely[:], sel_sum).then_inc(in_sel, 16)
            sync.dma_start(prm, perm).then_inc(in_sel, 16)
            sync.dma_start(xs[:], x).then_inc(in_x, 16)
            sync.dma_start(idn[:], ident).then_inc(in_moe, 16)
            sync.dma_start(sml[:], small).then_inc(in_moe, 16)
            sync.dma_start(selw32, sel_weight).then_inc(in_moe, 16)
            sync.dma_start(rw[:], route_w).then_inc(in_moe, 16)
            sync.dma_start(wg, w_gate_t).then_inc(in_ffn, 16)
            sync.dma_start(wu, w_up_t).then_inc(in_ffn, 16)
            sync.dma_start(wc[:, 0:HID // P, :], w_down_t).then_inc(in_ffn, 16)
            for p in range(NPASS):
                spread_bc(sync, p)
                for h in range(HV):
                    stack_parts(sync, p, h)
            for c in range(NCH):
                for i in range(2):
                    p = NCH + c
                    wait_read(sync, ("down", p, i))
                    t = TT * c + 2 * i
                    sync.dma_start(out[:, t:t + 2, :], xs[:, t:t + 2, :]).then_inc(stored, 16)
            sync.wait_ge(stored, 16 * 2 * NCH)

        @block.tensor
        def _(pe):
            def claim(use):
                b, n = USE[use]
                if n >= 1:
                    pe.wait_ge(bank_read[b], n)
                elif b >= 3:
                    pe.wait_ge(decayed, NBLK)
                    pe.wait_ge(scanned, NBLK)
                return gen[b]

            def done(ins, use):
                ins.then_inc(bank_full[USE[use][0]], 1)

            def spread_taps(lay):
                if lay == 0:
                    pe.wait_ge(in_taps, 16)
                    pe.wait_ge(zeroed, 1)
                for h in range(HV):
                    ps = claim(("spread_taps", lay, h))
                    done(nc.tensor.matmul(ps[:], ones[:], taps[:, lay * HV + h, :], start=True, stop=True),
                         ("spread_taps", lay, h))

            def conv(p, h, half):
                lay, c = divmod(p, NCH)
                if p == 0:
                    pe.wait_ge(in_ctx, 16 * NIN["ctx"])
                    pe.wait_ge(zeroed, 1)
                wait_read(pe, ("spread_taps", lay, h))
                ps = gen[USE[("conv", p, h)][0]] if half else claim(("conv", p, h))
                for k in range(DC // 2 * half, DC // 2 * (half + 1)):
                    last = nc.tensor.matmul(ps[:], wconv[:, lay * HV + h, k, :],
                                            ctxt[:, NB * c:NB * (c + 1), k:k + L], start=(k == 0), stop=(k == DC - 1))
                if half:
                    done(last, ("conv", p, h))

            def project_x(p):
                for h in range(HV):
                    wait_read(pe, ("conv", p, h))
                ps = claim(("project_x", p))
                for h in range(HV):
                    last = nc.tensor.matmul(ps[0:DR + 2 * DS, :], xpr[:, p // NCH, h, :], u[:, p, h, :],
                                            start=(h == 0), stop=(h == HV - 1))
                done(last, ("project_x", p))

            def project_dt(p):
                lay = p // NCH
                wait_read(pe, ("project_x", p))
                for h in range(HV):
                    ps = claim(("project_dt", p, h))
                    done(nc.tensor.matmul(ps[:], dtp[:, lay, h, :], xdbl[0:DR, :], start=True, stop=True),
                         ("project_dt", p, h))

            def spread(k, quantity, banks, ready):
                p, b = divmod(k, BP)
                h, i = divmod(b, BH)
                s, j = divmod(i, 4)
                if j == 0:
                    pe.wait_ge(stacked[h][s], 16 * NPART * (p + 1))
                nc.tensor.matmul(banks[k % 2][:], sels[:, j, :], stack[:, h, quantity, s, :],
                                 start=True, stop=True).then_inc(ready, 1)

            def delta_block(k):
                if k == 0:
                    pe.wait_ge(consts_made, 1)
                if k >= 2:
                    pe.wait_ge(decayed, k - 1)
                spread(k, 0, dps, delta_spread)

            def u_block(k):
                if k >= 2:
                    pe.wait_ge(scanned, k - 1)
                spread(k, 1, ups, u_spread)

            def sum_batch(m):
                half = m // 4
                p, h = divmod(half, HV)
                s = m % 4
                if s == 0:
                    if half >= 1:
                        pe.wait_ge(y_gated, half)
                    nc.tensor.matmul(yps[:], dperm[:, p // NCH, h, :], u[:, p, h, :],
                                     start=True, stop=False, skip_group_check=True)
                pe.wait_ge(c_weighted, 4 * m + 4)
                for j in range(4):
                    last = nc.tensor.matmul(yps[32 * j:32 * j + 32, :], sely[:, s, :], hst[:, (4 * m + j) % NHB, :],
                                            start=False, stop=(s == 3), skip_group_check=True)
                last.then_inc(y_summed, 1)

            def turn_y(p):
                if p == 0:
                    pe.wait_ge(in_moe, 16 * NIN["moe"])
                pe.wait_ge(y_gated, 2 * (p + 1))
                for i in range(2):
                    ps = claim(("turn_y", p, i))
                    for t in range(2):
                        for h in range(HV):
                            last = nc.tensor.transpose(ps[:, t * DX + h * P:t * DX + (h + 1) * P],
                                                       sz[:, h, (2 * i + t) * P:(2 * i + t + 1) * P], idn[:])
                    done(last, ("turn_y", p, i))

            def turn_x(p):
                pe.wait_ge(ffn_normed, p + 1)
                for k in range(KX):
                    ps = claim(("turn_x", p, k))
                    for t in range(TT):
                        last = nc.tensor.transpose(ps[:, t * P:(t + 1) * P], xn[:, t, k * P:(k + 1) * P], idn[:])
                    done(last, ("turn_x", p, k))

            def route(p):
                for k in range(KX):
                    wait_read(pe, ("turn_x", p, k))
                ps = claim(("route", p))
                for t in range(TT):
                    for k in range(KX):
                        last = nc.tensor.matmul(ps[:, t * NE:(t + 1) * NE], xnt[:, k, t * P:(t + 1) * P],
                                                rw[:, k, :], start=(k == 0), stop=(k == KX - 1))
                done(last, ("route", p))

            def turn_w(p):
                pe.wait_ge(weights_made, p - NCH + 1)
                ps = claim(("turn_w", p))
                for t in range(TT):
                    last = nc.tensor.transpose(ps[0:NPART * NE, t * P:(t + 1) * P],
                                               wprt[:, t].rearrange("p k e -> p (k e)"), idn[:])
                done(last, ("turn_w", p))

            def gate_or_up(p, t, which):
                if which == "gate" and t == 0:
                    for k in range(KX):
                        wait_read(pe, ("turn_x", p, k))
                    if p == 0:
                        pe.wait_ge(in_ffn, 16 * NIN["ffn"])
                if p == NCH and t == 0:
                    pe.wait_ge(in_w[which == "up"], 16)
                w = ((wg, wu) if p < NCH else (w1, w3))[which == "up"]
                ps = claim((which, p, t))
                for k in range(KX):
                    last = nc.tensor.matmul(ps[:], w[:, k, t * P:(t + 1) * P], xnt[:, k, :],
                                            start=(k == 0), stop=(k == KX - 1))
                done(last, (which, p, t))

            def weight(p, t):
                if t == 0:
                    pe.wait_ge(consts_made, 2)
                    wait_read(pe, ("turn_w", p))
                ps = claim(("weight", p, t))
                done(nc.tensor.matmul(ps[:], selw[:, t * P:(t + 1) * P], wts[:], start=True, stop=True),
                     ("weight", p, t))

            def down(p, t, part):
                n = tiles_of(p)
                i, o = divmod(t, 2)
                tiles = range(n // 2 * part, n if part else n // 2)
                if t == 0:
                    if p == NCH and part == 0:
                        pe.wait_ge(in_w[2], 16)
                    if weigh_on_pool(p):
                        pe.wait_ge(weighed, tiles[-1] + 1)
                    elif p >= NCH:
                        wait_read(pe, ("weight", p, tiles[-1]))
                    else:
                        for by_pool in (False, True):
                            mine = [j for j in tiles if hidden_on_pool(p, j) == by_pool]
                            if mine:
                                wait_hidden(pe, p, mine[-1])
                ps = gen[USE[("down", p, i)][0]] if o or part else claim(("down", p, i))
                for k in tiles:
                    last = nc.tensor.matmul(ps[:, o * DX:(o + 1) * DX], hid[:, k, t * P:(t + 1) * P],
                                            wc[:, k, :], start=(k == 0), stop=(k == n - 1))
                if o == 1 and part == 1:
                    done(last, ("down", p, i))

            for slot in SLOTS:
                if 0 <= slot + LEAD < NBLK:
                    delta_block(slot + LEAD)
                m, r = divmod(slot - SUMLAG, 4)
                if r == 0 and 0 <= m < NBLK // 4:
                    sum_batch(m)
                for kind, p, *at in AT.get(slot, []):
                    if kind == "spread_taps":
                        spread_taps(p)
                    elif kind == "conv":
                        conv(p, *at)
                    elif kind == "project_x":
                        project_x(p)
                    elif kind == "project_dt":
                        project_dt(p)
                    elif kind == "turn_y":
                        turn_y(p)
                    elif kind == "turn_x":
                        turn_x(p)
                    elif kind == "route":
                        route(p)
                    elif kind == "turn_w":
                        turn_w(p)
                    elif kind == "gate":
                        gate_or_up(p, at[0], "gate")
                    elif kind == "up":
                        gate_or_up(p, at[0], "up")
                    elif kind == "weight":
                        weight(p, at[0])
                    elif kind == "down":
                        down(p, *at)
                if 0 <= slot + 2 < NBLK:
                    u_block(slot + 2)

        @block.scalar
        def _(act):
            def conv_silu(p, h):
                ps = full(act, ("conv", p, h))
                ins = nc.scalar.activation(u[:, p, h, :], ps[:], ACT.Silu, bias=chan[:, p // NCH, h, 0:1])
                free(ins, ("conv", p, h))

            def keep_x(p):
                if p >= 1:
                    act.wait_ge(b_spread[(p - 1) % 2], 16 * EB * ((p - 1) // 2 + 1))
                    act.wait_ge(c_spread[(p - 1) % 2], 16 * EB * ((p - 1) // 2 + 1))
                ps = full(act, ("project_x", p))
                free(nc.scalar.activation(xdbl[:], ps[0:DR + 2 * DS, :], ACT.Copy), ("project_x", p))

            def dt_bias(p):
                if p >= 1:
                    for h in range(HV):
                        act.wait_ge(delta_ready[h], p)
                for h in range(HV):
                    ps = full(act, ("project_dt", p, h))
                    free(nc.scalar.activation(dtv[:, h * CH:(h + 1) * CH], ps[:], ACT.Identity,
                                              bias=chan[:, p // NCH, h, 1:2]), ("project_dt", p, h))

            def dt_abs(p):
                for h in range(HV):
                    wait_read(act, ("project_dt", p, h))
                if p >= 1:
                    for h in range(HV):
                        act.wait_ge(lost_ready[h], p)
                nc.scalar.activation(dtt[:], dtv[:], ACT.Abs).then_inc(abs_ready, 1)

            def dt_exp(p):
                act.wait_ge(abs_ready, p + 1)
                nc.scalar.activation(dtt[:], dtt[:], ACT.Exp, scale=-1.0).then_inc(exp_ready, 1)

            def dt_ln(p):
                act.wait_ge(exp_ready, p + 1)
                if p >= 1:
                    for h in range(HV):
                        act.wait_ge(log_summed[h], p)
                nc.scalar.activation(dtl[:], dtt[:], ACT.Ln, bias=1.0).then_inc(ln_ready, 1)

            def hi(p, q, h):
                if q == 0:
                    act.wait_ge(delta_ready[h], p + 1)
                else:
                    act.wait_ge(delta_u_ready[h], p + 1)
                if p >= 1:
                    for s in range(4):
                        act.wait_ge(stacked[h][s], 16 * NPART * p)
                nc.scalar.activation(parts[:, 0, q, h, :], val[:, q, h, :], ACT.Copy).then_inc(hi_ready[h], 1)

            def mid(p, q, h):
                act.wait_ge(rest_ready[h], order(p, q))
                nc.scalar.activation(parts[:, 1, q, h, :], val[:, q, h, :], ACT.Copy).then_inc(mid_ready[h], 1)

            def decay(k):
                p, b = divmod(k, BP)
                if k == 0:
                    act.wait_ge(a_made, 1)
                    act.wait_ge(zeroed, 2)
                if k >= NDA:
                    act.wait_ge(scanned, k - NDA + 1)
                act.wait_ge(delta_spread, k + 1)
                nc.scalar.activation(da[:, k % NDA, :, 1:], dps[k % 2][:].rearrange("p (b l) -> p b l", b=NB)[:, :, 1:],
                                     ACT.Exp, scale=aneg[:, p // NCH, b:b + 1]).then_inc(decayed, 1)

            def fetch(p, i):
                w, to, use = ((w1_t, w1, ("gate", p, HID // P - 1)), (w3_t, w3, ("up", p, HID // P - 1)),
                              (w2_t, wc[:], ("down", p, 1)))[i]
                full(act, use)
                act.dma_start(to, w).then_inc(in_w[i], 16)

            def gate_silu(p):
                act.wait_ge(gate_shift, p + 1)
                if p >= 1:
                    full(act, ("turn_y", p - 1, 1))
                for t in range(TT):
                    b, h = divmod(t, HV)
                    nc.scalar.activation(sz[:, h, b * L:(b + 1) * L], xs[:, TT * (p % NCH) + t, :], ACT.Silu,
                                         bias=shift[:, t:t + 1], scale=rstd[0][:, t:t + 1]).then_inc(gate_ready, 1)

            def keep_xt(p):
                for k in range(KX):
                    ps = full(act, ("turn_x", p, k))
                    ins = nc.scalar.activation(xnt[:, k, :], ps[:], ACT.Copy)
                    free(ins, ("turn_x", p, k))

            def tanh(p, t):
                n = first_tile(p) + t
                ps = full(act, ("gate", p, t))
                if n >= 2:
                    wait_hidden(act, *tile_use("up", n - 2)[1:])
                nc.scalar.activation(th[:, n % 2, :], ps[:], ACT.Tanh, scale=0.5).then_inc(tanh_ready, 1)

            def keep_up(p, t):
                i = pool_tiles(p, t) - 1
                if i >= 2:
                    act.wait_ge(pool_hidden, i - 1)
                ps = full(act, ("up", p, t))
                free(nc.scalar.activation(upc[:, i % 2, :], ps[:], ACT.Copy, scale=0.5), ("up", p, t))

            def keep_weight(p, t):
                if t >= 2:
                    act.wait_ge(weighed, t - 1)
                ps = full(act, ("weight", p, t))
                free(nc.scalar.activation(wgt[:, t % 2, :], ps[:], ACT.Copy), ("weight", p, t))

            act.wait_ge(in_sel, 16 * NIN["sel"])
            nc.scalar.activation(aneg[:], alog[:], ACT.Exp).then_inc(a_exp, 1)
            for slot in SLOTS:
                if 0 <= slot + LEAD < NBLK:
                    decay(slot + LEAD)
                for kind, p, *at in AT.get(slot, []):
                    if kind == "conv_silu":
                        conv_silu(p, *at)
                    elif kind == "keep_x":
                        keep_x(p)
                    elif kind == "dt_bias":
                        dt_bias(p)
                    elif kind == "dt_abs":
                        dt_abs(p)
                    elif kind == "dt_exp":
                        dt_exp(p)
                    elif kind == "dt_ln":
                        dt_ln(p)
                    elif kind == "hi":
                        hi(p, *at)
                    elif kind == "mid":
                        mid(p, *at)
                    elif kind == "fetch":
                        fetch(p, at[0])
                    elif kind == "gate_silu":
                        gate_silu(p)
                    elif kind == "keep_xt":
                        keep_xt(p)
                    elif kind == "keep_up":
                        keep_up(p, at[0])
                    elif kind == "keep_weight":
                        keep_weight(p, at[0])
                    elif kind == "tanh":
                        tanh(p, at[0])
                    elif kind == "route_exp":
                        act.wait_ge(routed, p - NCH + 1)
                        nc.scalar.activation(e21[:], d21[:], ACT.Exp).then_inc(route_expd, 1)
                    elif kind == "keep_w":
                        ps = full(act, ("turn_w", p))
                        ins = nc.scalar.activation(wts[:], ps[0:NPART * NE, :], ACT.Copy)
                        free(ins, ("turn_w", p))

        @block.vector
        def _(dve):
            steps = [0]

            def then(ins):
                steps[0] += 1
                ins.then_inc(dve_step, 1)
                dve.wait_ge(dve_step, steps[0])

            def scale_taps(lay):
                for h in range(HV):
                    ps = full(dve, ("spread_taps", lay, h))
                    ins = nc.vector.tensor_tensor(wconv[:, lay * HV + h], ps[:].rearrange("p (k e) -> p k e", k=DC),
                                                  inp[:, lay, h, :].unsqueeze(1).to_broadcast([P, DC, P]), ALU.mult)
                    free(ins, ("spread_taps", lay, h))

            def round_up(p):
                dve.wait_ge(exp_ready, p + 1)
                if p >= 1:
                    for h in range(HV):
                        dve.wait_ge(delta_ready[h], p)
                nc.vector.tensor_scalar(dta[:], dtt[:], 1.0, -1.0, ALU.add, ALU.add).then_inc(rounded, 1)

            def delta(p, h):
                dve.wait_ge(log_summed[h], p + 1)
                if p >= 1:
                    dve.wait_ge(lo_ready[h], order(p - 1, 0))
                nc.vector.scalar_tensor_tensor(out=val[:, 0, h, :], in0=dtv[:, h * CH:(h + 1) * CH], scalar=0.0,
                                               in1=dta[:, h * CH:(h + 1) * CH], op0=ALU.max, op1=ALU.add)\
                    .then_inc(delta_ready[h], 1)

            def times_b(k):
                p = k // BP
                dve.wait_ge(u_spread, k + 1)
                if k % BP == 0:
                    dve.wait_ge(b_spread[p % 2], 16 * EB * (p // 2 + 1))
                nc.vector.tensor_tensor(ups[k % 2][:], ups[k % 2][:], brep[:, p % 2, :], ALU.mult)\
                    .then_inc(weighted, 1)

            def scan(k):
                dve.wait_ge(decayed, k + 1)
                dve.wait_ge(weighted, k + 1)
                if k >= NHB:
                    dve.wait_ge(y_summed, (k - NHB) // 4 + 1)
                nc.vector.tensor_tensor_scan(hst[:, k % NHB, :], da[:, k % NDA].rearrange("p b l -> p (b l)"),
                                             ups[k % 2][:], 0.0, ALU.mult, ALU.add).then_inc(scanned, 1)

            def gate_y(half):
                p, h = divmod(half, HV)
                dve.wait_ge(y_summed, 4 * half + 4)
                dve.wait_ge(gate_ready, TT * (p + 1))
                nc.vector.tensor_tensor(sz[:, h, :], yps[:], sz[:, h, :], ALU.mult).then_inc(y_gated, 1)

            def stats(which, c):
                for i in range(TT):
                    nc.vector.bn_stats(bns[which][:, i, :], xs[:, TT * c + i, :]).then_inc(stats_made[which], 1)

            def aggregate(which, n):
                for i in range(TT):
                    dve.wait_ge(stats_made[which], TT * n + i + 1)
                    nc.vector.bn_aggr(mv[which][:, i, :], bns[which][:, i, :]).then_inc(aggregated[which], 1)
                dve.wait_ge(aggregated[which], TT * (n + 1))
                nc.vector.tensor_scalar(ve[which][:], mv[which][:, :, 1], EPS, None, ALU.add)\
                    .then_inc(var_ready[which], 1)

            def gate_stats(p):
                if p == 0:
                    dve.wait_ge(in_x, 16 * NIN["x"])
                if p >= NCH:
                    for i in range(2):
                        wait_read(dve, ("down", p - NCH, i))
                stats(0, p % NCH)

            def gate_shift_of(p):
                dve.wait_ge(rstd_ready[0], p + 1)
                if p >= 1:
                    dve.wait_ge(gate_ready, TT * p)
                nc.vector.scalar_tensor_tensor(out=shift[:], in0=mv[0][:, :, 0], scalar=-1.0, in1=rstd[0][:],
                                               op0=ALU.mult, op1=ALU.mult).then_inc(gate_shift, 1)

            def add_y(p):
                c = p % NCH
                for i in range(2):
                    ps = full(dve, ("turn_y", p, i))
                    t = TT * c + 2 * i
                    rows = xs[:, t:t + 2, :].rearrange("p a b -> p (a b)")
                    dve.wait_ge(gate_ready, TT * (p + 1))
                    ins = nc.vector.tensor_tensor(rows, ps[:], rows, ALU.add)
                    free(ins, ("turn_y", p, i))

            def ffn_stats(p):
                for i in range(2):
                    wait_read(dve, ("turn_y", p, i))
                stats(1, p % NCH)

            def ffn_norm(p):
                c = p % NCH
                dve.wait_ge(rstd_ready[1], p + 1)
                if p >= 1 and pool_tiles(p - 1, None):
                    dve.wait_ge(pool_hidden, pool_tiles(p - 1, None))
                for t in range(TT):
                    ins = nc.vector.tensor_scalar(xn[:, t, :], xs[:, TT * c + t, :], mv[1][:, t, 0:1],
                                                  rstd[1][:, t:t + 1], ALU.subtract, ALU.mult)
                ins.then_inc(ffn_normed, 1)

            def silu(p, t):
                n = first_tile(p) + t
                dve.wait_ge(tanh_ready, n + 1)
                ps = full(dve, ("gate", p, t))
                ins = nc.vector.scalar_tensor_tensor(out=th[:, n % 2, :], in0=th[:, n % 2, :], scalar=1.0, in1=ps[:],
                                                     op0=ALU.add, op1=ALU.mult)
                free(ins, ("gate", p, t))

            def hidden(p, t):
                n = first_tile(p) + t
                wait_net(dve, p, t)
                wait_read(dve, ("gate", p, t))
                ps = full(dve, ("up", p, t))
                ins = nc.vector.scalar_tensor_tensor(out=hid[:, t, :], in0=th[:, n % 2, :], scalar=0.5, in1=ps[:],
                                                     op0=ALU.mult, op1=ALU.mult)
                free(ins, ("up", p, t))

            def weigh(p, t):
                wait_hidden(dve, p, t)
                ps = full(dve, ("weight", p, t))
                free(nc.vector.tensor_tensor(hid[:, t, :], ps[:], hid[:, t, :], ALU.mult), ("weight", p, t))

            def add_down(p, i):
                ps = full(dve, ("down", p, i))
                t = TT * (p % NCH) + 2 * i
                rows = xs[:, t:t + 2, :].rearrange("p a b -> p (a b)")
                ins = nc.vector.tensor_tensor(rows, ps[:], rows, ALU.add)
                free(ins, ("down", p, i))

            def top2(p):
                ps = full(dve, ("route", p))
                ins = nc.vector.tensor_copy(lg[:].rearrange("p t e -> p (t e)"), ps[:, 0:TT * NE])
                free(ins, ("route", p))
                wait_read(dve, ("route", p))
                for t in range(TT):
                    ins = nc.vector.max(top[:, t, :], lg[:, t, :])
                then(ins)
                for t in range(TT):
                    ins = nc.vector.max_index(tix[:, t, :], top[:, t, :], lg[:, t, :])
                then(ins)
                then(nc.vector.tensor_copy(tif[:], tix[:, :, 0:2]))
                nc.vector.tensor_tensor(d21[:], top[:, :, 1], top[:, :, 0], ALU.subtract).then_inc(routed, 1)

            def route_weights(p):
                dve.wait_ge(route_expd, p - NCH + 1)
                then(nc.vector.tensor_scalar(s21[:], e21[:], 1.0, None, ALU.add))
                then(nc.vector.reciprocal(p1[:], s21[:]))
                then(nc.vector.tensor_tensor(p2[:], e21[:], p1[:], ALU.mult))
                for t in range(TT):
                    nc.vector.tensor_scalar(m1[:, t, :], sml[:, 0:NE], tif[:, t, 0:1], p1[:, t:t + 1],
                                            ALU.is_equal, ALU.mult)
                    ins = nc.vector.tensor_scalar(m2[:, t, :], sml[:, 0:NE], tif[:, t, 1:2], p2[:, t:t + 1],
                                                  ALU.is_equal, ALU.mult)
                then(ins)
                then(nc.vector.tensor_tensor(wtok[:], m1[:], m2[:], ALU.add))
                left = wtok[:]
                for k in range(NPART):
                    then(nc.vector.tensor_copy(whb[:, :, k, :], left))
                    if k < NPART - 1:
                        then(nc.vector.tensor_tensor(wr[:, :, k, :], left, whb[:, :, k, :], ALU.subtract))
                        left = wr[:, :, k, :]
                nc.vector.tensor_copy(wprt[:], whb[:]).then_inc(weights_made, 1)

            def make_constants():
                dve.wait_ge(in_ctx, 16 * NIN["ctx"])
                dve.wait_ge(in_sel, 16 * NIN["sel"])
                nc.vector.tensor_copy(sels[:], sels32)
                for lay in range(2):
                    for h in range(HV):
                        ins = nc.vector.tensor_scalar(dperm[:, lay, h, :], prm, chan[:, lay, h, 2:3], None, ALU.mult)
                ins.then_inc(consts_made, 1)
                dve.wait_ge(a_exp, 1)
                nc.vector.tensor_scalar(aneg[:], aneg[:], -1.0, None, ALU.mult).then_inc(a_made, 1)
                dve.wait_ge(in_moe, 16 * NIN["moe"])
                nc.vector.tensor_copy(selw[:], selw32).then_inc(consts_made, 1)

            nc.vector.memset(ones[:], 1.0)
            nc.vector.memset(ctxt[:, :, 0:DC - 1], 0.0).then_inc(zeroed, 1)
            nc.vector.memset(da[:, :, :, 0:1], 0.0).then_inc(zeroed, 1)
            dve.wait_ge(in_proj, 16)
            for slot in SLOTS:
                if 0 <= slot < NBLK:
                    scan(slot)
                if 0 <= slot + 1 < NBLK:
                    times_b(slot + 1)
                half, r = divmod(slot - BH - 4, BH)
                if r == 0 and 0 <= half < NBLK // BH:
                    gate_y(half)
                if slot == CONSTS:
                    make_constants()
                for kind, p, *at in AT.get(slot, []):
                    if kind == "scale_taps":
                        scale_taps(p)
                    elif kind == "round_up":
                        round_up(p)
                    elif kind == "delta":
                        delta(p, at[0])
                    elif kind == "lost" and on_vector(p, at[0]):
                        lost(dve, nc.vector, p, at[0])
                    elif kind == "log_sum" and on_vector(p, at[0]):
                        log_sum(dve, nc.vector, p, at[0])
                    elif kind == "delta_u" and on_vector(p, at[0]):
                        delta_u(dve, nc.vector, p, at[0])
                    elif kind == "rest" and on_vector(p, at[1]):
                        rest(dve, nc.vector, p, *at)
                    elif kind == "lo" and on_vector(p, at[1]):
                        lo(dve, nc.vector, p, *at)
                    elif kind == "gate_stats":
                        gate_stats(p)
                    elif kind == "gate_aggr":
                        aggregate(0, p)
                    elif kind == "ffn_stats":
                        ffn_stats(p)
                    elif kind == "ffn_aggr":
                        aggregate(1, p)
                    elif kind == "gate_shift":
                        gate_shift_of(p)
                    elif kind == "add_y":
                        add_y(p)
                    elif kind == "ffn_norm":
                        ffn_norm(p)
                    elif kind == "top2":
                        top2(p)
                    elif kind == "route_w":
                        route_weights(p)
                    elif kind == "silu":
                        silu(p, at[0])
                    elif kind == "hidden" and not hidden_on_pool(p, at[0]):
                        hidden(p, at[0])
                    elif kind == "weigh" and not weigh_on_pool(p):
                        weigh(p, at[0])
                    elif kind == "add_down":
                        add_down(p, at[0])

        @block.gpsimd
        def _(pool):
            def times_c(k):
                p = k // BP
                pool.wait_ge(scanned, k + 1)
                if k % BP == 0:
                    pool.wait_ge(c_spread[p % 2], 16 * EB * (p // 2 + 1))
                nc.gpsimd.tensor_tensor(hst[:, k % NHB, :], hst[:, k % NHB, :], crep[:, p % 2, :], ALU.mult)\
                    .then_inc(c_weighted, 1)

            def hidden(p, t):
                n = first_tile(p) + t
                wait_net(pool, p, t)
                wait_read(pool, ("gate", p, t))
                wait_read(pool, ("up", p, t))
                nc.gpsimd.tensor_tensor(hid[:, t, :], th[:, n % 2, :], upc[:, (pool_tiles(p, t) - 1) % 2, :],
                                        ALU.mult).then_inc(pool_hidden, 1)

            def weigh(p, t):
                wait_hidden(pool, p, t)
                wait_read(pool, ("weight", p, t))
                nc.gpsimd.tensor_tensor(hid[:, t, :], wgt[:, t % 2, :], hid[:, t, :], ALU.mult)\
                    .then_inc(weighed, 1)

            def power(which, n):
                pool.wait_ge(var_ready[which], n + 1)
                if n == 0 and which == 0:
                    pool.wait_ge(in_moe, 16 * NIN["moe"])
                nc.gpsimd.tensor_tensor(rstd[which][:], ve[which][:], sml[:, NE:NE + TT], ALU.pow)\
                    .then_inc(rstd_ready[which], 1)

            for slot in SLOTS:
                if 0 <= slot < NBLK:
                    times_c(slot)
                for kind, p, *at in AT.get(slot, []):
                    if kind == "gate_rstd":
                        power(0, p)
                    elif kind == "ffn_rstd":
                        power(1, p)
                    elif kind == "hidden" and hidden_on_pool(p, at[0]):
                        hidden(p, at[0])
                    elif kind == "weigh" and weigh_on_pool(p):
                        weigh(p, at[0])
                    elif kind == "lost" and not on_vector(p, at[0]):
                        lost(pool, nc.gpsimd, p, at[0])
                    elif kind == "log_sum" and not on_vector(p, at[0]):
                        log_sum(pool, nc.gpsimd, p, at[0])
                    elif kind == "delta_u" and not on_vector(p, at[0]):
                        delta_u(pool, nc.gpsimd, p, at[0])
                    elif kind == "rest" and not on_vector(p, at[1]):
                        rest(pool, nc.gpsimd, p, *at)
                    elif kind == "lo" and not on_vector(p, at[1]):
                        lo(pool, nc.gpsimd, p, *at)


def kernel(**inputs):
    import concourse.bacc as bacc
    from concourse.bass_utils import run_bass_kernel_spmd

    a = {k: np.ascontiguousarray(v) for k, v in inputs.items()}
    f = np.float32
    q = np.arange(P)
    chan_of_q = 32 * (q // 8 % 4) + 8 * (q // 32) + q % 8
    order = np.concatenate([h * P + chan_of_q for h in range(HV)])
    layers = ("L0_xattn_", "L1_xattn_")

    def stacked(name, lay_out):
        return np.stack([lay_out(a[n + name]) for n in layers])

    def rows(w):
        return w[order].reshape(HV, P, -1).transpose(1, 0, 2)

    def k_tiles(w):
        return w.reshape(-1, P, w.shape[-1]).transpose(1, 0, 2)

    def by_block(w):
        return w[order].reshape(HV * BH, EB * DS).T

    arrays = {
        "x": k_tiles(a["x"].reshape(TOK, DX)),
        "ctx_t": a["ctx_1024"].reshape(TOK, DM).T,
        "in_proj_t": stacked("in_proj_w", lambda w: w[order].reshape(HV, P, DM).transpose(2, 0, 1)).transpose(1, 0, 2, 3),
        "conv_w": stacked("conv_w", lambda w: w.reshape(DI, DC)[order].reshape(HV, P, DC).transpose(0, 2, 1)).reshape(
            1, 2 * HV, DC * P),
        "channel": np.stack([np.concatenate([rows(a[n + m].reshape(DI, 1)) for m in ("conv_b", "dt_proj_b", "D")],
                                            axis=-1) for n in layers], axis=1),
        "x_proj_t": stacked("x_proj_w", lambda w: rows(w.T)).transpose(1, 0, 2, 3),
        "dt_proj_t": stacked("dt_proj_w", lambda w: w[order].reshape(HV, P, DR).transpose(2, 0, 1)).transpose(1, 0, 2, 3),
        "a_log": stacked("A_log", by_block).transpose(1, 0, 2),
        "w_gate_t": k_tiles(a["L0_ffn_w_gate"].T),
        "w_up_t": k_tiles(a["L0_ffn_w_up"].T),
        "w_down_t": k_tiles(a["L0_ffn_w_down"].T),
        "route_w": k_tiles(a["L1_ffn_gate_w"]),
        "w1_t": k_tiles(a["L1_ffn_w1"].transpose(1, 0, 2).reshape(DX, MOE)),
        "w3_t": k_tiles(a["L1_ffn_w3"].transpose(1, 0, 2).reshape(DX, MOE)),
        "w2_t": k_tiles(a["L1_ffn_w2"].reshape(MOE, DX)),
    }
    r = np.arange(NPART * 32)
    arrays["sel_spread"] = np.stack([(r[:, None] % 32 == EB * j + q[None, :] // DS) for j in range(4)], 1).astype(f)
    arrays["sel_sum"] = np.stack([(EB * s + q[:, None] // DS == np.arange(32)[None, :]) for s in range(4)], 1).astype(f)
    arrays["perm"] = (chan_of_q[:, None] == q[None, :]).astype(f)
    arrays["ident"] = np.eye(P, dtype=f)
    arrays["sel_weight"] = (np.arange(NPART * NE)[:, None] % NE == np.arange(MOE)[None, :] // EI).astype(f)
    arrays["small"] = np.concatenate([np.tile(np.arange(NE, dtype=f), (P, 1)), np.full((P, TT), -0.5, f)], axis=1)

    nc = bacc.Bacc("TRN2", target_bir_lowering=False, num_devices=1)
    arrays = {k: np.ascontiguousarray(v) for k, v in arrays.items()}
    args = [nc.dram_tensor(k, v.shape, mybir.dt.float32, kind="ExternalInput").ap() for k, v in arrays.items()]
    out = nc.dram_tensor("out", (P, TOK // P, DX), mybir.dt.float32, kind="ExternalOutput").ap()
    build(nc, *args, out)
    got = run_bass_kernel_spmd(nc, [arrays], core_ids=[0]).results[0]["out"]
    return np.ascontiguousarray(got.transpose(1, 0, 2)).reshape(B, L, DX)
```
